# Optimizing a Trainium2 kernel written in Bass

```python
import numpy as np
import jax
import jax.numpy as jnp

def _softmax(x, axis=-1):
    return jax.nn.softmax(x, axis=axis)

def _gelu(x):
    return jax.nn.gelu(x, approximate=True)

def _silu(x):
    return jax.nn.silu(x)

def _sigmoid(x):
    return jax.nn.sigmoid(x)

def _layernorm(x, axis=-1, eps=1e-05):
    m = jnp.mean(x, axis=axis, keepdims=True)
    v = jnp.var(x, axis=axis, keepdims=True)
    return (x - m) / jnp.sqrt(v + eps)

def _scatter_add(tgt, idx, src, axis=0):
    return tgt.at[idx].add(src)

def _segment_sum(src, seg, n):
    return jax.ops.segment_sum(src, seg, n)
kernel_name = 'mk_seq_postln_d1_jaxref_r4_8824c0'

def setup_inputs(seed: int=0):
    np.random.seed(seed)
    _w = jnp.asarray

    def _L0_attn_setup():
        import jax, jax.numpy as jnp
        import numpy as np
        D_MODEL = 256
        NUM_HEADS = 16
        HEAD_DIM = D_MODEL // NUM_HEADS
        EPS = 1e-08
        key = jax.random.key(seed)
        ks = jax.random.split(key, 6)
        B, T = (4, 512)
        s = 0.02
        return {'x': jax.random.normal(ks[0], (B, T, D_MODEL), dtype=jnp.float32), 'Wq': jax.random.normal(ks[1], (D_MODEL, D_MODEL), dtype=jnp.float32) * s, 'Wk': jax.random.normal(ks[2], (D_MODEL, D_MODEL), dtype=jnp.float32) * s, 'Wv': jax.random.normal(ks[3], (D_MODEL, D_MODEL), dtype=jnp.float32) * s, 'Wo': jax.random.normal(ks[4], (D_MODEL, D_MODEL), dtype=jnp.float32) * s, 'bo': jnp.zeros((D_MODEL,), dtype=jnp.float32)}
    _L0_attn_in = _L0_attn_setup()

    def _L0_ffn_setup():
        import jax, jax.numpy as jnp
        import numpy as np
        DIM = 256
        HIDDEN = 768
        SCALE = 1.0 / 127.0

        def _dequant(w_int, dtype):
            return w_int.astype(dtype) * jnp.asarray(SCALE, dtype)
        key = jax.random.key(seed)
        k_x, k_g, k_u, k_d = jax.random.split(key, 4)
        x = jax.random.normal(k_x, (4, 512, DIM), dtype=jnp.float32)
        w_gate = jax.random.randint(k_g, (HIDDEN, DIM), -127, 128, dtype=jnp.int32)
        w_up = jax.random.randint(k_u, (HIDDEN, DIM), -127, 128, dtype=jnp.int32)
        w_down = jax.random.randint(k_d, (DIM, HIDDEN), -127, 128, dtype=jnp.int32)
        return {'x': x, 'w_gate': w_gate, 'w_up': w_up, 'w_down': w_down}
    _L0_ffn_in = _L0_ffn_setup()
    _d = {'L0_attn_x': _L0_attn_in['x'], 'L0_attn_Wq': _L0_attn_in['Wq'], 'L0_attn_Wk': _L0_attn_in['Wk'], 'L0_attn_Wv': _L0_attn_in['Wv'], 'L0_attn_Wo': _L0_attn_in['Wo'], 'L0_attn_bo': _L0_attn_in['bo'], 'L0_ffn_w_gate': _L0_ffn_in['w_gate'], 'L0_ffn_w_up': _L0_ffn_in['w_up'], 'L0_ffn_w_down': _L0_ffn_in['w_down']}
    _x0 = _d['L0_attn_x']
    _d['L0_attn_x'] = jax.random.normal(jax.random.fold_in(jax.random.key(seed), 1), (8, 512, 256), dtype=_x0.dtype)
    del _x0
    return _d

def reference(L0_attn_x, L0_attn_Wq, L0_attn_Wk, L0_attn_Wv, L0_attn_Wo, L0_attn_bo, L0_ffn_w_gate, L0_ffn_w_up, L0_ffn_w_down):

    def _L0_attn_ref(x, Wq, Wk, Wv, Wo, bo):
        import jax, jax.numpy as jnp
        import numpy as np
        D_MODEL = 256
        NUM_HEADS = 16
        HEAD_DIM = D_MODEL // NUM_HEADS
        EPS = 1e-08
        B, T, _ = x.shape
        H, D = (NUM_HEADS, HEAD_DIM)
        scale = jnp.sqrt(jnp.asarray(D, dtype=x.dtype))
        q = (x @ Wq.T).reshape(B, T, H, D).transpose(0, 2, 1, 3)
        k = (x @ Wk.T).reshape(B, T, H, D).transpose(0, 2, 1, 3)
        v = (x @ Wv.T).reshape(B, T, H, D).transpose(0, 2, 1, 3)
        s = jnp.einsum('bhtd,bhsd->bhts', q, k) / scale
        m = jnp.max(s, axis=-1, keepdims=True)
        e = jnp.exp(s - m)
        num = jnp.einsum('bhts,bhsd->bhtd', e, v)
        den = jnp.sum(e, axis=-1, keepdims=True) + EPS
        out = (num / den).transpose(0, 2, 1, 3).reshape(B, T, H * D)
        return out @ Wo.T + bo

    def _L0_ffn_ref(x, w_gate, w_up, w_down):
        import jax, jax.numpy as jnp
        import numpy as np
        DIM = 256
        HIDDEN = 768
        SCALE = 1.0 / 127.0

        def _dequant(w_int, dtype):
            return w_int.astype(dtype) * jnp.asarray(SCALE, dtype)
        wg = _dequant(w_gate, x.dtype)
        wu = _dequant(w_up, x.dtype)
        wd = _dequant(w_down, x.dtype)
        gate = jnp.einsum('bsd,hd->bsh', x, wg)
        up = jnp.einsum('bsd,hd->bsh', x, wu)
        h = jax.nn.silu(gate) * up
        return jnp.einsum('bsh,dh->bsd', h, wd)
    x = L0_attn_x
    x = _layernorm(x + _L0_attn_ref(x, L0_attn_Wq, L0_attn_Wk, L0_attn_Wv, L0_attn_Wo, L0_attn_bo), axis=-1)
    x = _layernorm(x + _L0_ffn_ref(x, L0_ffn_w_gate, L0_ffn_w_up, L0_ffn_w_down), axis=-1)
    return x

_drawn_inputs = setup_inputs


def setup_inputs(seed=0):
    import zlib

    import numpy as np

    out = dict(_drawn_inputs(seed))
    spreads = {'L0_attn_bo': (0.0, 0.29)}
    factors = {'L0_attn_Wq': 8.0, 'L0_attn_Wk': 8.0, 'L0_attn_Wv': 8.0, 'L0_attn_Wo': 8.0}
    for name, (base, spread) in spreads.items():
        noise = np.random.default_rng([zlib.crc32(name.encode()), seed]).standard_normal(out[name].shape)
        drawn = base * np.exp(spread * noise) if base else spread * noise
        out[name] = jnp.asarray(drawn.astype(out[name].dtype))
    for name, factor in factors.items():
        out[name] = (out[name] * factor).astype(out[name].dtype)
    return out
```

```python
from contextlib import ExitStack

import concourse.bass as bass
from concourse import mybir

F32 = mybir.dt.float32
F32R = mybir.dt.float32r
BF16 = mybir.dt.bfloat16
I32 = mybir.dt.int32
ACT = mybir.ActivationFunctionType
ALU = mybir.AluOpType
AX = mybir.AxisListType

P = 128
NB, T, D = 8, 512, 256
H, DH = 16, 16
HID = 768
TT = T // P
CT = D // P
NH = HID // P
QUADS = H // 4
SLOTS = H * TT
Q_TERMS = (0, 0, 0, 1, 1, 2)
K_TERMS = (0, 1, 2, 0, 1, 0)
KQ = 16 * len(Q_TERMS)
KM = KQ + 3
RING = 2
EPS_DEN = 1e-8
EPS_LN = 1e-5
W_SCALE = 1.0 / 127.0

S_V = (1, 2)
S_XT = (5, 8)
S_QK = (12, 19, 26, 33)
S_TURN = (3, 4, 6, 7)
S_BACK = (10, 11)
S_OUT = (14, 15)
S_X1T = (23, 24)
S_UP = tuple(28 + 4 * n for n in range(NH))
S_DOWN = (57, 60)
MLAG = 6
PVLAG = 3

RM_ORDER = []
for _s in range(SLOTS):
    RM_ORDER.append(("tile", _s))
    if _s >= 16 and _s % 16 == MLAG - 1:
        RM_ORDER.append(("turn", _s // 16 - 1))
RM_ORDER.append(("turn", QUADS - 1))
RM_AT = {key: n for n, key in enumerate(RM_ORDER)}
RM_PER = len(RM_ORDER)

W_TASKS = 4 + 3 * 3


def layer_program(nc, x, wq, wk, wv, wo, bo, wg, wu, wd, out):
    with ExitStack() as ctx:
        def sb(name, shape, dt):
            return ctx.enter_context(nc.sbuf_tensor(name, shape, dt))

        def sem(name):
            return ctx.enter_context(nc.semaphore(name))

        ident = sb("ident", [P, P], F32)
        identb = sb("identb", [P, P], BF16)
        wqT, wkT, wvT, woT = (sb(n, [P, CT, D], F32) for n in ("wqT", "wkT", "wvT", "woT"))
        wgT = sb("wgT", [P, CT, HID], F32R)
        wuT = sb("wuT", [P, CT, HID], F32R)
        wdT = sb("wdT", [P, NH, D], F32R)
        bo_rows = sb("bo_rows", [P, D], F32)
        minus_half = sb("minus_half", [P, TT], F32)
        eps_ln = sb("eps_ln", [P, TT], F32)
        zeros = sb("zeros", [P, T], BF16)
        x_in = sb("x_in", [P, TT, D], F32)
        xT = sb("xT", [P, CT, T], F32)
        parts = sb("parts", [P, 4, 3, T], BF16)
        rest = sb("rest", [P, 2, T], F32)
        qs = [sb(f"qs{n}", [KM, H, T], BF16) for n in range(2)]
        ks = [sb(f"ks{n}", [KM, H, T], BF16) for n in range(2)]
        v1 = [sb(f"v1_{n}", [P, TT, H, 2 * DH], F32) for n in range(2)]
        negmax = sb("negmax", [P, 2, 4, TT], F32)
        mrest = sb("mrest", [P, 2, 16], F32)
        mparts = sb("mparts", [P, 2, 64], BF16)
        mrows = sb("mrows", [P, P], BF16)
        e = sb("e", [P, RING, 4, T], F32)
        oT = sb("oT", [P, QUADS, T], F32)
        den = sb("den", [P, 2, H], F32)
        rden = sb("rden", [P, 2, H], F32)
        att = sb("att", [P, TT, D], F32)
        attT = sb("attT", [P, CT, T], F32)
        res = sb("res", [P, TT, D], F32)
        stats = sb("stats", [P, 2, TT, 6], F32)
        mv = sb("mv", [P, 2, TT, 2], F32)
        veps = sb("veps", [P, 2, TT], F32)
        rstd = sb("rstd", [P, 2, TT], F32)
        x1h = sb("x1h", [P, CT, T], F32R)
        x1l = sb("x1l", [P, CT, T], F32R)
        th = attT
        hf = sb("hf", [P, 2, T], F32)
        hh = sb("hh", [P, NH, T], F32R)
        hl = sb("hl", [P, NH, T], F32R)
        y = att
        w_stage = oT[:, :, :].rearrange("p q (a c) -> p q a c", a=2)
        i_stage = [e[:, :, :, :].rearrange("p r j t -> p (r j t)")[:, k * 1536:(k + 1) * 1536] for k in range(2)]
        i_stage.append(y[:, :, :].rearrange("p a c -> p (a c)"))

        rm_ps = ctx.enter_context(nc.psum_tensor("rm_ps", [P, 2, T], F32))
        sc_ps = ctx.enter_context(nc.psum_tensor("sc_ps", [P, 2, T], F32))
        pv_ps = ctx.enter_context(nc.psum_tensor("pv_ps", [P, T], F32))
        pr_ps = ctx.enter_context(nc.psum_tensor("pr_ps", [P, T], F32))
        fi_ps = ctx.enter_context(nc.psum_tensor("fi_ps", [P, 2, T], F32))

        w_in = [sem(f"w_in{n}") for n in range(2)]
        w_flt = sem("w_flt")
        ready = sem("ready")
        ready_d = sem("ready_d")
        w_done = sem("w_done")
        x_landed = sem("x_landed")
        bo_landed = sem("bo_landed")
        pr_full = sem("pr_full")
        xt_done = sem("xt_done")
        p1_done, r_done, p2_done, p3_done = sem("p1_done"), sem("r_done"), sem("p2_done"), sem("p3_done")
        stacked = [sem(f"stacked{q}") for q in range(QUADS)]
        v_done = sem("v_done")
        rm_full, rm_free = sem("rm_full"), sem("rm_free")
        m_step, m_split = sem("m_step"), sem("m_split")
        mrow_in = [sem(f"mrow_in{q}") for q in range(QUADS)]
        sc_full, exp_done = sem("sc_full"), sem("exp_done")
        pv_done, ot_done = sem("pv_done"), sem("ot_done")
        fi_full = [sem(f"fi_full{k}") for k in range(2)]
        norm_step, att_done, attT_done = sem("norm_step"), sem("att_done"), sem("attT_done")
        res_landed, res_bo = sem("res_landed"), sem("res_bo")
        r1_done, r2_done = sem("r1_done"), sem("r2_done")
        st_done, mv_done = sem("st_done"), sem("mv_done")
        ve_done, rs_done = sem("ve_done"), sem("rs_done")
        x1_done, x1h_done, x1l_done = sem("x1_done"), sem("x1h_done"), sem("x1l_done")
        th_done, pg_done, hf_done, hh_done, hl_done = (
            sem("th_done"), sem("pg_done"), sem("hf_done"), sem("hh_done"), sem("hl_done"))
        y_done, stored = sem("y_done"), sem("stored")

        def fi_tasks(bank, b, k):
            return b * 12 + (W_TASKS + 1 - bank) // 2 + k // 2

        def iterations(eng, body):
            live = lambda i: (i + 2 < NB, 0 <= i + 1 < NB, 0 <= i < NB, 0 <= i - 1 < NB)
            for i in range(-2, 2):
                body(i, i % 2, live(i), i)
            end = 2 + (NB - 4) // 2 * 2
            with eng.Fori(1, end // 2) as pair:
                body(2 * pair, 0, (True,) * 4, 2)
                body(2 * pair + 1, 1, (True,) * 4, 3)
            for i in range(end, NB + 1):
                body(i, i % 2, live(i), i)

        block = ctx.enter_context(nc.Block())

        @block.sync
        def _(sp):
            for k, w in enumerate((wq, wk, wv, wo)):
                sp.dma_start(w_stage[:, k], w.rearrange("(a p) c -> p a c", p=P)).then_inc(w_in[0], 16)
            sp.dma_start(x_in[:, :, :], x[0].rearrange("(t p) c -> p t c", p=P)).then_inc(x_landed, 16)
            for stage, w in zip(i_stage[:2], (wg, wu)):
                sp.dma_start(stage.bitcast(I32).rearrange("p (a c) -> p a c", c=D),
                             w.rearrange("(a p) c -> p a c", p=P)).then_inc(w_in[1], 16)
            for k in range(2):
                dst = i_stage[2][:, 0:768] if k == 0 else res[:, :, :].rearrange("p a c -> p (a c)")[:, 0:768]
                sp.dma_start(dst.bitcast(I32), wd[k * P:(k + 1) * P, :]).then_inc(w_in[1], 16)
            sp.dma_start(bo_rows[:, :], bo.rearrange("(a n) -> a n", a=1).broadcast_to([P, D])).then_inc(bo_landed, 16)

            def stack(b, par, Q):
                at = 64 * (Q % 2)
                for which, dst, terms in ((0, qs, Q_TERMS), (1, ks, K_TERMS)):
                    for n, part in enumerate(terms):
                        src = parts[at:at + 64, 2 * (Q // 2) + which, part, :]
                        sp.dma_start(dst[par][16 * n:16 * n + 16, 4 * Q:4 * Q + 4, :], src)\
                          .then_inc(stacked[Q], 16)

            def body(i, par, live, n):
                project, rowmax, attend, finish = live

                def mrow(Q):
                    sp.wait_ge(rm_free, RM_PER * (i + 1) + RM_AT["turn", Q] + 1)
                    sp.dma_start(qs[1 - par][KQ:KM, 4 * Q:4 * Q + 4, :], mrows[64 * (Q % 2):64 * (Q % 2) + 48, :])\
                      .then_inc(mrow_in[Q], 16)

                if project and n > -2:
                    sp.wait_ge(pr_full, 8 * (i + 1) + 2)
                    sp.dma_start(x_in[:, :, :], x[i + 2].rearrange("(t p) c -> p t c", p=P)).then_inc(x_landed, 16)
                if finish:
                    if n > 1:
                        sp.wait_ge(r2_done, 2 * (i - 1))
                    else:
                        sp.wait_ge(w_done, W_TASKS)
                    sp.dma_start(res[:, :, :], x[i - 1].rearrange("(t p) c -> p t c", p=P)).then_inc(res_landed, 16)
                if n >= 2:
                    store(i - 2)
                if rowmax:
                    mrow(0)
                    mrow(1)
                for Q in range(QUADS):
                    if rowmax and Q >= 2:
                        mrow(Q)
                    if project:
                        if not rowmax:
                            sp.wait_ge(p3_done, 4 * (i + 2) + 2 * (Q // 2) + 2)
                        if attend:
                            sp.wait_ge(sc_full, SLOTS * i + 16 * (Q + 1))
                        stack(i + 2, par, Q)

            def store(b):
                sp.wait_ge(y_done, 2 * b + 2)
                sp.dma_start(out[b].rearrange("(t p) c -> p t c", p=P), y[:, :, :]).then_inc(stored, 16)

            iterations(sp, body)
            store(NB - 1)
            sp.wait_ge(stored, 16 * NB)

        @block.gpsimd
        def _(pool):
            nc.gpsimd.memset(ident[:, :], 0.0).then_inc(ready, 1)
            pool.wait_ge(ready, 1)
            nc.gpsimd.affine_select(out=ident[:, :], in_=ident[:, :], compare_op=ALU.not_equal, fill=1.0,
                                    base=0, pattern=[[-1, P]], channel_multiplier=1).then_inc(ready, 1)
            nc.gpsimd.memset(minus_half[:, :], -0.5)
            nc.gpsimd.memset(eps_ln[:, :], EPS_LN)
            nc.gpsimd.memset(zeros[:, :], 0.0)
            nc.gpsimd.memset(mparts[:, :, :], 0.0).then_inc(ready, 1)
            for n in range(2):
                nc.gpsimd.memset(v1[n][:, :, :, DH:], 1.0).then_inc(ready, 1)

            pool.wait_ge(ready, 5)

            def split(b, m):
                pool.wait_ge(r_done, 4 * b + m + 1)
                nc.gpsimd.tensor_tensor(parts[:, m, 1, :], rest[:, m % 2, :], zeros[:, :], ALU.add).then_inc(p2_done, 1)
                pool.wait_ge(p2_done, 4 * b + m + 1)
                nc.gpsimd.tensor_tensor(parts[:, m, 2, :], rest[:, m % 2, :], parts[:, m, 1, :],
                                        ALU.subtract).then_inc(p3_done, 1)

            def max_parts(b, Q, n):
                k = Q % 2
                step = 3 * (QUADS * b + Q)
                m = negmax[:, k].rearrange("p j t -> p (j t)")
                pool.wait_ge(rm_free, RM_PER * b + RM_AT["tile", 16 * Q + 15] + 1)
                nc.gpsimd.tensor_tensor(mparts[:, k, 0:16], m, zeros[:, 0:16], ALU.add).then_inc(m_step, 1)
                pool.wait_ge(m_step, step + 1)
                nc.gpsimd.tensor_tensor(mrest[:, k, :], m, mparts[:, k, 0:16], ALU.subtract).then_inc(m_step, 1)
                pool.wait_ge(m_step, step + 2)
                nc.gpsimd.tensor_tensor(mparts[:, k, 16:32], mrest[:, k, :], zeros[:, 0:16], ALU.add).then_inc(m_step, 1)
                pool.wait_ge(m_step, step + 3)
                nc.gpsimd.tensor_tensor(mparts[:, k, 32:48], mrest[:, k, :], mparts[:, k, 16:32],
                                        ALU.subtract).then_inc(m_split, 1)

            def rsqrt(b, k):
                pool.wait_ge(mv_done, 2 * b + k + 1)
                nc.gpsimd.tensor_tensor(veps[:, k, :], mv[:, k, :, 1], eps_ln[:, :], ALU.add).then_inc(ve_done, 1)
                pool.wait_ge(ve_done, 2 * b + k + 1)
                nc.gpsimd.tensor_tensor(rstd[:, k, :], veps[:, k, :], minus_half[:, :], ALU.pow).then_inc(rs_done, 1)

            def body(i, par, live, n):
                project, rowmax, attend, finish = live
                for s in range(SLOTS + 1):
                    if finish and s == 0:
                        if n == 1:
                            pool.wait_ge(bo_landed, 16)
                        pool.wait_ge(res_landed, 16 * i)
                        for t in range(TT):
                            last = nc.gpsimd.tensor_tensor(res[:, t, :], res[:, t, :], bo_rows[:, :], ALU.add)
                        last.then_inc(res_bo, 1)
                    if finish and s == S_OUT[1] + 5:
                        rsqrt(i - 1, 0)
                    if project and s - 4 in S_QK:
                        split(i + 2, S_QK.index(s - 4))
                    if rowmax and s and s % 16 == 0:
                        max_parts(i + 1, s // 16 - 1, n)
                    if finish and s - 7 in S_UP:
                        k = S_UP.index(s - 7)
                        pool.wait_ge(hh_done, NH * (i - 1) + k + 1)
                        nc.gpsimd.tensor_tensor(hl[:, k, :], hf[:, k % 2, :], hh[:, k, :].bitcast(F32),
                                                ALU.subtract).then_inc(hl_done, 1)
                if finish:
                    rsqrt(i - 1, 1)

            iterations(pool, body)

        @block.scalar
        def _(act):
            def copy(dst, src):
                return nc.scalar.activation(dst, src, ACT.Copy)

            def weights(n0, n1):
                for n in range(n0, n1):
                    act.wait_ge(fi_full[n % 2], n // 2 + 1)
                    bank = fi_ps[:, n % 2, :]
                    if n < 2:
                        for c in range(CT):
                            last = copy((wqT, wkT)[n][:, c, :].rearrange("p (q d j) -> p q j d", q=QUADS, j=4),
                                        bank[:, c * D:(c + 1) * D].rearrange("p (q j d) -> p q j d", q=QUADS, j=4))
                        last.then_inc(w_done, 1)
                        continue
                    if n < 4:
                        dst = (wvT, woT)[n - 2][:, :, :]
                        bank = bank.rearrange("p (c o) -> p c o", c=CT)
                    elif n < 10:
                        r = (n - 4) % 3
                        dst = (wgT if n < 7 else wuT)[:, :, 256 * r:256 * r + 256]
                        bank = bank.rearrange("p (c o) -> p c o", c=CT)
                    else:
                        dst = wdT[:, 2 * (n - 10):2 * (n - 10) + 2, :]
                        bank = bank.rearrange("p (a o) -> p a o", a=2)
                    copy(dst, bank).then_inc(w_done, 1)

            def body(i, par, live, n):
                project, rowmax, attend, finish = live
                if n == -2:
                    weights(0, 4)
                if n == -1:
                    weights(4, W_TASKS)
                for s in range(SLOTS):
                    if attend:
                        j, kt, Q = s % 4, s // 4 % TT, s // 16
                        if j == 0 and (n > 0 or s // 4 >= RING):
                            act.wait_ge(pv_done, 16 * i + s // 4 - RING + 1)
                        act.wait_ge(sc_full, SLOTS * i + s + 1)
                        nc.scalar.activation(e[:, s // 4 % RING, j, :], sc_ps[:, s % 2, :], ACT.Exp, scale=0.25)\
                            .then_inc(exp_done, 1)
                        if s >= 16 + PVLAG and s % 16 == PVLAG + 1:
                            ot_copy(i, s // 16 - 1, n)
                    if rowmax and s - 1 in S_V:
                        k = S_V.index(s - 1)
                        act.wait_ge(pr_full, 8 * (i + 1) + 6 + k + 1)
                        if n == -1 and k == 0:
                            act.wait_ge(ready, 5)
                        copy(v1[1 - par][:, 2 * k:2 * k + 2, :, 0:DH],
                             pr_ps[:, :].rearrange("p (t h d) -> p t h d", t=2, h=H)).then_inc(v_done, 1)
                    if project and s - 1 in S_XT:
                        k = S_XT.index(s - 1)
                        act.wait_ge(pr_full, 8 * (i + 2) + k + 1)
                        copy(xT[:, k, :], pr_ps[:, :]).then_inc(xt_done, 1)
                    if project and s - 2 in S_QK:
                        m = S_QK.index(s - 2)
                        act.wait_ge(pr_full, 8 * (i + 2) + 3 + m)
                        if n > -2:
                            for Q in (2 * (m // 2), 2 * (m // 2) + 1):
                                act.wait_ge(stacked[Q], 192 * (i + 2))
                        copy(parts[:, m, 0, :], pr_ps[:, :]).then_inc(p1_done, 1)
                    if finish and s - 1 in S_BACK:
                        k = S_BACK.index(s - 1)
                        act.wait_ge(fi_full[k], fi_tasks(k, i - 1, 4) + 1)
                        copy(attT[:, k, :], fi_ps[:, k, :]).then_inc(attT_done, 1)
                    if finish and s - 1 in S_X1T:
                        k = S_X1T.index(s - 1)
                        act.wait_ge(fi_full[k], fi_tasks(k, i - 1, 8) + 1)
                        copy(x1h[:, k, :], fi_ps[:, k, :]).then_inc(x1h_done, 1)
                    if finish and s - 2 in S_UP:
                        k = S_UP.index(s - 2)
                        act.wait_ge(fi_full[0], fi_tasks(0, i - 1, 10 + 2 * k) + 1)
                        if k >= 2 or n > 1:
                            act.wait_ge(hf_done, NH * (i - 1) + k - 1)
                        nc.scalar.activation(th[:, k % 2, :], fi_ps[:, 0, :], ACT.Tanh, scale=0.5 * W_SCALE)\
                            .then_inc(th_done, 1)
                    if finish and s - 6 in S_UP:
                        k = S_UP.index(s - 6)
                        act.wait_ge(hf_done, NH * (i - 1) + k + 1)
                        copy(hh[:, k, :], hf[:, k % 2, :]).then_inc(hh_done, 1)
                if attend:
                    ot_copy(i, QUADS - 1, n)

            def ot_copy(i, Q, n):
                act.wait_ge(pv_done, 16 * i + 4 * Q + 4)
                if Q == 0 and n > 0:
                    act.wait_ge(att_done, TT * i)
                copy(oT[:, Q, :], pv_ps[:, :]).then_inc(ot_done, 1)

            iterations(act, body)

        @block.vector
        def _(dve):
            dve.wait_ge(ready, 2)
            nc.vector.tensor_copy(identb[:, :], ident[:, :]).then_inc(ready_d, 1)
            for n in range(2):
                nc.vector.memset(ks[n][KQ:KM, :, :], 1.0).then_inc(ready_d, 1)

            def stats_of(b, k, src, t0):
                for t in (t0, t0 + 1):
                    last = nc.vector.bn_stats(stats[:, k, t, :], src[:, t, :])
                last.then_inc(st_done, 1)

            def mean_var(b, k):
                for t in range(TT):
                    last = nc.vector.bn_aggr(mv[:, k, t, :], stats[:, k, t, :])
                last.then_inc(mv_done, 1)

            def normalise(b, k, buf, done):
                dve.wait_ge(rs_done, 2 * b + k + 1)
                for t in range(TT):
                    last = nc.vector.tensor_scalar(buf[:, t, :], buf[:, t, :], mv[:, k, t, 0:1], rstd[:, k, t:t + 1],
                                                   ALU.subtract, ALU.mult)
                    if k and t == 1:
                        last.then_inc(done, 1)
                last.then_inc(done, 1)

            def body(i, par, live, n):
                project, rowmax, attend, finish = live
                b = i - 1
                if n == -1:
                    dve.wait_ge(w_in[1], 64)
                    for stage in (i_stage[0], i_stage[1], i_stage[2][:, 0:768],
                                  res[:, :, :].rearrange("p a c -> p (a c)")[:, 0:768]):
                        nc.vector.tensor_copy(stage, stage.bitcast(I32)).then_inc(w_flt, 1)
                for s in range(SLOTS):
                    if finish and s == S_OUT[1] + 4:
                        dve.wait_ge(st_done, 4 * b + 2)
                    if rowmax:
                        j, t, Q = s // TT % 4, s % TT, s // 16
                        at = RM_AT["tile", s]
                        dve.wait_ge(rm_full, RM_PER * (i + 1) + at + 1)
                        if s % 16 == 0 and (Q >= 2 or n > -1):
                            dve.wait_ge(m_split, QUADS * (i + 1) + Q - 1)
                        nc.vector.tensor_reduce(negmax[:, Q % 2, j, t:t + 1], rm_ps[:, at % 2, :], AX.X, ALU.max,
                                                negate=True).then_inc(rm_free, 1)
                        if s >= 16 and s % 16 == MLAG - 1:
                            if project and Q == 2:
                                dve.wait_ge(p3_done, 4 * (i + 2) + 2)
                            if project and Q == 3:
                                dve.wait_ge(p3_done, 4 * (i + 2) + 4)
                            m_out(i, Q - 1, n)
                    if project and s - 3 in S_QK:
                        m = S_QK.index(s - 3)
                        dve.wait_ge(p1_done, 4 * (i + 2) + m + 1)
                        if m >= 2 or n > -2:
                            dve.wait_ge(p3_done, 4 * (i + 2) + m - 1)
                        nc.vector.tensor_tensor(rest[:, m % 2, :], pr_ps[:, :], parts[:, m, 0, :],
                                                ALU.subtract).then_inc(r_done, 1)
                    if not finish:
                        continue
                    if s - 1 in S_TURN:
                        t = S_TURN.index(s - 1)
                        bank = fi_ps[:, t % 2, :].rearrange("p (h c) -> p h c", c=2 * DH)
                        dve.wait_ge(fi_full[t % 2], fi_tasks(t % 2, b, t) + 1)
                        nc.vector.tensor_scalar(den[:, t % 2, :], bank[:, :, DH], EPS_DEN, None, ALU.add)\
                            .then_inc(norm_step, 1)
                        dve.wait_ge(norm_step, 8 * b + 2 * t + 1)
                        nc.vector.reciprocal(rden[:, t % 2, :], den[:, t % 2, :]).then_inc(norm_step, 1)
                        dve.wait_ge(norm_step, 8 * b + 2 * t + 2)
                        if t == 0 and n > 1:
                            dve.wait_ge(stored, 16 * b)
                        nc.vector.tensor_tensor(att[:, t, :].rearrange("p (h d) -> p h d", d=DH), bank[:, :, 0:DH],
                                                rden[:, t % 2, :].unsqueeze(2).broadcast_to([P, H, DH]),
                                                ALU.mult).then_inc(att_done, 1)
                    if s - 2 in S_OUT:
                        k = S_OUT.index(s - 2)
                        dve.wait_ge(fi_full[k], fi_tasks(k, b, 6) + 1)
                        if k == 0:
                            dve.wait_ge(res_bo, b + 1)
                        half = res[:, 2 * k:2 * k + 2, :].rearrange("p a c -> p (a c)")
                        nc.vector.tensor_tensor(half, fi_ps[:, k, :], half, ALU.add).then_inc(r1_done, 1)
                    if s == S_OUT[1] + 3:
                        for k in range(2):
                            dve.wait_ge(r1_done, 2 * b + k + 1)
                            stats_of(b, 0, res, 2 * k)
                    if s == S_OUT[1] + 4:
                        mean_var(b, 0)
                    if s == S_OUT[1] + 6:
                        normalise(b, 0, res, x1_done)
                    if s - 2 in S_X1T:
                        k = S_X1T.index(s - 2)
                        dve.wait_ge(x1h_done, CT * b + k + 1)
                        nc.vector.tensor_tensor(x1l[:, k, :], fi_ps[:, k, :], x1h[:, k, :].bitcast(F32),
                                                ALU.subtract).then_inc(x1l_done, 1)
                    if s - 3 in S_UP:
                        k = S_UP.index(s - 3)
                        dve.wait_ge(th_done, NH * b + k + 1)
                        nc.vector.scalar_tensor_tensor(th[:, k % 2, :], th[:, k % 2, :], 1.0, fi_ps[:, 0, :],
                                                       ALU.add, ALU.mult).then_inc(pg_done, 1)
                    if s - 5 in S_UP:
                        k = S_UP.index(s - 5)
                        dve.wait_ge(fi_full[1], fi_tasks(1, b, 11 + 2 * k) + 1)
                        dve.wait_ge(pg_done, NH * b + k + 1)
                        if k >= 2 or n > 1:
                            dve.wait_ge(hl_done, NH * b + k - 1)
                        nc.vector.tensor_tensor(hf[:, k % 2, :], fi_ps[:, 1, :], th[:, k % 2, :],
                                                ALU.mult).then_inc(hf_done, 1)
                    if s - 2 in S_DOWN:
                        down(i, b, S_DOWN.index(s - 2), n)
                if finish:
                    for k in range(2):
                        if S_DOWN[k] + 2 >= SLOTS:
                            down(i, b, k, n)
                    for k in range(2):
                        dve.wait_ge(r2_done, 2 * b + k + 1)
                        stats_of(b, 1, y, 2 * k)
                    dve.wait_ge(st_done, 4 * b + 4)
                if rowmax:
                    m_out(i, QUADS - 1, n)
                if finish:
                    mean_var(b, 1)
                    normalise(b, 1, y, y_done)

            def down(i, b, k, n):
                dve.wait_ge(fi_full[k], fi_tasks(k, b, 22) + 1)
                nc.vector.scalar_tensor_tensor(
                    y[:, 2 * k:2 * k + 2, :].rearrange("p a c -> p (a c)"), fi_ps[:, k, :], 0.5 * W_SCALE ** 3,
                    res[:, 2 * k:2 * k + 2, :].rearrange("p a c -> p (a c)"), ALU.mult, ALU.add).then_inc(r2_done, 1)

            def m_out(i, Q, n):
                at = RM_AT["turn", Q]
                dve.wait_ge(rm_full, RM_PER * (i + 1) + at + 1)
                if Q >= 2 or n > -1:
                    dve.wait_ge(mrow_in[(Q + 2) % 4], 16 * (i + 1) + (16 if Q >= 2 else 0))
                r = 64 * (Q % 2)
                nc.vector.tensor_copy(mrows[r:r + 48, :], rm_ps[:, at % 2, :].bitcast(BF16)[r:r + 48, 0:P])\
                    .then_inc(rm_free, 1)

            iterations(dve, body)

        @block.tensor
        def _(pe):
            mm = nc.tensor.matmul

            def weights(n0, n1):
                for n in range(n0, n1):
                    if n >= 2:
                        pe.wait_ge(w_done, n - 1)
                    bank = fi_ps[:, n % 2, :]
                    for c in range(4):
                        if n < 4:
                            src = w_stage[:, n, c % 2, (c // 2) * P:(c // 2 + 1) * P]
                        elif n < 10:
                            r = (n - 4) % 3
                            src = i_stage[(n - 4) // 3].rearrange("p (a c) -> p a c", c=D)[
                                :, 2 * r + c % 2, (c // 2) * P:(c // 2 + 1) * P]
                        else:
                            half = (i_stage[2], res[:, :, :].rearrange("p a c -> p (a c)"))[c % 2]
                            hid = 2 * (n - 10) + c // 2
                            src = half[:, hid * P:(hid + 1) * P]
                        last = nc.tensor.transpose(bank[:, c * P:(c + 1) * P], src, ident[:, :])
                    last.then_inc(fi_full[n % 2], 1)

            def body(i, par, live, n):
                project, rowmax, attend, finish = live
                b = i - 1
                if n == -2:
                    pe.wait_ge(ready, 2)
                    pe.wait_ge(w_in[0], 64)
                    weights(0, 4)
                    pe.wait_ge(w_done, 4)
                if n == -1:
                    pe.wait_ge(w_flt, 4)
                    weights(4, W_TASKS)
                for s in range(SLOTS):
                    if rowmax:
                        j, t, Q = s // TT % 4, s % TT, s // 16
                        at = RM_AT["tile", s]
                        if s % 16 == 0:
                            pe.wait_ge(stacked[Q], 192 * (i + 2))
                        if n > -1 or at >= 2:
                            pe.wait_ge(rm_free, RM_PER * (i + 1) + at - 1)
                        q_, k_ = qs[1 - par], ks[1 - par]
                        h = 4 * Q + j
                        mm(rm_ps[:, at % 2, :], q_[0:KQ, h, t * P:(t + 1) * P], k_[0:KQ, h, :],
                           start=True, stop=True).then_inc(rm_full, 1)
                        if s >= 16 and s % 16 == MLAG - 1:
                            m_turn(i, Q - 1, n)
                    if attend:
                        j, kt, Q = s % 4, s // 4 % TT, s // 16
                        h = 4 * Q + j
                        if n == 0 and s == 0:
                            pe.wait_ge(ready, 5)
                            pe.wait_ge(ready_d, 3)
                        if s % 16 == 0:
                            pe.wait_ge(mrow_in[Q], 16 * (i + 1))
                        if n > 0 or s >= 2:
                            pe.wait_ge(exp_done, SLOTS * i + s - 1)
                        mm(sc_ps[:, s % 2, :], ks[par][0:KM, h, kt * P:(kt + 1) * P], qs[par][0:KM, h, :],
                           start=True, stop=True).then_inc(sc_full, 1)
                        if s >= 4 and s % 4 == (3 + PVLAG) % 4 and s >= 3 + PVLAG:
                            product(i, par, (s - 3 - PVLAG) // 4, n)
                    if rowmax and s in S_V:
                        k = S_V.index(s)
                        if k == 0:
                            pe.wait_ge(r_done, 4 * (i + 2))
                        else:
                            pe.wait_ge(v_done, 2 * (i + 1) + k)
                        for t in (2 * k, 2 * k + 1):
                            for c in range(CT):
                                last = mm(pr_ps[:, (t % 2) * D:(t % 2 + 1) * D], xT[:, c, t * P:(t + 1) * P],
                                          wvT[:, c, :], start=(c == 0), stop=(c == CT - 1))
                        last.then_inc(pr_full, 1)
                    if project and s in S_XT:
                        k = S_XT.index(s)
                        if k == 0:
                            pe.wait_ge(x_landed, 16 * (i + 3))
                            if n > -2:
                                pe.wait_ge(v_done, 2 * (i + 2))
                        else:
                            pe.wait_ge(xt_done, CT * (i + 2) + k)
                        for t in range(TT):
                            last = nc.tensor.transpose(pr_ps[:, t * P:(t + 1) * P], x_in[:, t, k * P:(k + 1) * P],
                                                       ident[:, :])
                        last.then_inc(pr_full, 1)
                    if project and s in S_QK:
                        m = S_QK.index(s)
                        if m == 0:
                            pe.wait_ge(xt_done, CT * (i + 3))
                        else:
                            pe.wait_ge(r_done, 4 * (i + 2) + m)
                        w = (wqT, wkT)[m % 2]
                        for c in range(CT):
                            last = mm(pr_ps[:, :], w[:, c, (m // 2) * P:(m // 2 + 1) * P], xT[:, c, :],
                                      start=(c == 0), stop=(c == CT - 1))
                        last.then_inc(pr_full, 1)
                    if not finish:
                        continue
                    if s in S_TURN:
                        t = S_TURN.index(s)
                        if t == 0:
                            pe.wait_ge(ot_done, QUADS * i)
                        if t >= 2:
                            pe.wait_ge(att_done, TT * b + t - 1)
                        elif n > 1:
                            pe.wait_ge(r2_done, 2 * (b - 1) + t + 1)
                        elif t == 0:
                            pe.wait_ge(w_done, W_TASKS)
                        for Q in range(QUADS):
                            last = nc.tensor.transpose(fi_ps[:, t % 2, Q * P:(Q + 1) * P], oT[:, Q, t * P:(t + 1) * P],
                                                       ident[:, :])
                        last.then_inc(fi_full[t % 2], 1)
                    if s in S_BACK:
                        c = S_BACK.index(s)
                        pe.wait_ge(att_done, TT * b + TT)
                        for t in range(TT):
                            last = nc.tensor.transpose(fi_ps[:, c, t * P:(t + 1) * P], att[:, t, c * P:(c + 1) * P],
                                                       ident[:, :])
                        last.then_inc(fi_full[c], 1)
                    if s in S_OUT:
                        k = S_OUT.index(s)
                        if k == 0:
                            pe.wait_ge(attT_done, CT * b + CT)
                        for t in (2 * k, 2 * k + 1):
                            for c in range(CT):
                                last = mm(fi_ps[:, k, (t % 2) * D:(t % 2 + 1) * D], attT[:, c, t * P:(t + 1) * P],
                                          woT[:, c, :], start=(c == 0), stop=(c == CT - 1))
                        last.then_inc(fi_full[k], 1)
                    if s in S_X1T:
                        c = S_X1T.index(s)
                        pe.wait_ge(x1_done, b + 1)
                        for t in range(TT):
                            last = nc.tensor.transpose(fi_ps[:, c, t * P:(t + 1) * P], res[:, t, c * P:(c + 1) * P],
                                                       ident[:, :])
                        last.then_inc(fi_full[c], 1)
                    if s in S_UP or s - 2 in S_UP:
                        bank = int(s not in S_UP)
                        k = S_UP.index(s - 2 * bank)
                        if k == 0:
                            pe.wait_ge(x1l_done, CT * b + CT)
                        else:
                            pe.wait_ge((pg_done, hf_done)[bank], NH * b + k)
                        first = True
                        for xpart in (x1l, x1h):
                            for c in range(CT):
                                last = mm(fi_ps[:, bank, :], (wgT, wuT)[bank][:, c, k * P:(k + 1) * P], xpart[:, c, :],
                                          start=first, stop=(xpart is x1h and c == CT - 1))
                                first = False
                        last.then_inc(fi_full[bank], 1)
                    if s in S_DOWN:
                        k = S_DOWN.index(s)
                        if k == 0:
                            pe.wait_ge(hl_done, NH * b + NH)
                        for t in (2 * k, 2 * k + 1):
                            for g in range(NH):
                                for hpart in (hl, hh):
                                    last = mm(fi_ps[:, k, (t % 2) * D:(t % 2 + 1) * D], hpart[:, g, t * P:(t + 1) * P],
                                              wdT[:, g, :], start=(g == 0 and hpart is hl),
                                              stop=(g == NH - 1 and hpart is hh))
                        last.then_inc(fi_full[k], 1)
                if attend:
                    product(i, par, 15, n)
                if rowmax:
                    m_turn(i, QUADS - 1, n)

            def m_turn(i, Q, n):
                at = RM_AT["turn", Q]
                pe.wait_ge(m_split, QUADS * (i + 1) + Q + 1)
                pe.wait_ge(rm_free, RM_PER * (i + 1) + at - 1)
                if n == -1 and Q == 0:
                    pe.wait_ge(ready_d, 1)
                nc.tensor.transpose(rm_ps[:, at % 2, :].bitcast(BF16)[:, 0:P],
                                    mparts[:, :, :].rearrange("p a m -> p (a m)"), identb[:, :]).then_inc(rm_full, 1)

            def product(i, par, g, n):
                Q, kt = g // TT, g % TT
                if g == 0:
                    pe.wait_ge(v_done, 2 * (i + 1))
                if kt == 0 and (Q or n > 0):
                    pe.wait_ge(ot_done, QUADS * i + Q)
                pe.wait_ge(exp_done, SLOTS * i + 4 * g + 4)
                for j in range(4):
                    last = mm(pv_ps[32 * j:32 * j + 32, :], v1[par][:, kt, 4 * Q + j, :], e[:, g % RING, j, :],
                              start=(kt == 0), stop=(kt == TT - 1), tile_position=(0, 32 * j))
                last.then_inc(pv_done, 1)

            iterations(pe, body)


_INS = ["L0_attn_x", "L0_attn_Wq", "L0_attn_Wk", "L0_attn_Wv", "L0_attn_Wo", "L0_attn_bo",
        "L0_ffn_w_gate", "L0_ffn_w_up", "L0_ffn_w_down"]


def kernel(**inputs):
    import numpy as _np
    import concourse.bacc as _bacc
    from concourse import mybir as _mybir
    from concourse.bass_utils import run_bass_kernel_spmd as _run

    nc = _bacc.Bacc("TRN2", target_bir_lowering=False, num_devices=1)
    arrays, args = {}, []
    for name in _INS:
        a = _np.ascontiguousarray(inputs[name])
        arrays[f"in_{name}_dram"] = a
        args.append(nc.dram_tensor(f"in_{name}_dram", a.shape, _mybir.dt.from_np(a.dtype), kind="ExternalInput").ap())
    out = nc.dram_tensor("out_0_dram", (NB, T, D), _mybir.dt.float32, kind="ExternalOutput").ap()
    layer_program(nc, *args, out)
    r = _run(nc, [arrays], core_ids=[0])
    return r.results[0]["out_0_dram"]
```

```python
from contextlib import ExitStack

import concourse.bass as bass
from concourse import mybir

F32 = mybir.dt.float32
F32R = mybir.dt.float32r
BF16 = mybir.dt.bfloat16
I32 = mybir.dt.int32
ACT = mybir.ActivationFunctionType
ALU = mybir.AluOpType
AX = mybir.AxisListType

P = 128
NB, T, D = 8, 512, 256
H, DH = 16, 16
HID = 768
TT = T // P
CT = D // P
NH = HID // P
QUADS = H // 4
SLOTS = H * TT
Q_TERMS = (0, 0, 0, 1, 1, 2)
K_TERMS = (0, 1, 2, 0, 1, 0)
KQ = 16 * len(Q_TERMS)
KM = KQ + 3
RING = 2
EPS_DEN = 1e-8
EPS_LN = 1e-5
W_SCALE = 1.0 / 127.0

LEAD = 28
PVLAG = 3
MLAG = 6

S_XT = (0, 3)
S_QK = (7, 11, 19, 26)
S_QK2 = (8, 12, 20, 27)
S_V = (15, 16, 23, 24)
S_TURN = (1, 1, 5, 5)
S_DIVIDE = (2, 3, 6, 7)
S_BACK = (9, 9)
S_OUT = (13, 15, 16, 17)
S_X1T = (28, 28)
FREE = [_s for _s in range(31, SLOTS) if _s % 4 != 2]
S_UP = FREE[0:18]
S_DOWN = (FREE[18], FREE[18], FREE[19], FREE[19], FREE[20],
          FREE[21], FREE[21], FREE[22], FREE[22], FREE[23])

PR_AT = {("xt", 0): 0, ("xt", 1): 1}
for _s, _key in sorted([(S_QK2[m], ("qk", m)) for m in range(4)] + [(S_V[2 * k + 1], ("v", k)) for k in range(2)]):
    PR_AT[_key] = len(PR_AT)

RM_ORDER = []
for _s in range(SLOTS):
    RM_ORDER.append(("tile", _s))
    if _s % 16 == MLAG - 1:
        RM_ORDER.append(("turn", (_s // 16 - 1) % QUADS))
RM_AT = {key: n for n, key in enumerate(RM_ORDER)}
RM_PER = len(RM_ORDER)


def rm_at(nb, key):
    if nb == NB:
        return -1
    return RM_AT[key] - (nb > 0 or RM_AT[key] > MLAG)


def turn_at(b, nb, Q):
    if Q < QUADS - 1:
        return b, rm_at(nb, ("turn", Q))
    return b + 1, rm_at(nb + 1, ("turn", Q))


def project_slot(n, s):
    if n >= 0 or s < S_V[0]:
        return s
    return s - (SLOTS - LEAD - 6 - S_V[0]) if s >= SLOTS - LEAD - 6 else -9


def rowmax_of(i, n, s):
    ahead, tile = divmod(s + LEAD, SLOTS)
    return i + ahead, n + ahead, tile


W_TASKS = 4 + 3 * 3
W_SLOTS = {5: (0, 2), 13: (2, 4)}
W_SLOTS.update({SLOTS - LEAD + 3 + _n: (4 + _n, 5 + _n) for _n in range(W_TASKS - 4)})


def layer_program(nc, x, wq, wk, wv, wo, bo, wg, wu, wd, out):
    with ExitStack() as ctx:
        def sb(name, shape, dt):
            return ctx.enter_context(nc.sbuf_tensor(name, shape, dt))

        def sem(name):
            return ctx.enter_context(nc.semaphore(name))

        ident = sb("ident", [P, P], F32)
        identb = sb("identb", [P, P], BF16)
        wqT, wkT, wvT, woT = (sb(n, [P, 2, CT, D], F32R) for n in ("wqT", "wkT", "wvT", "woT"))
        wgT = sb("wgT", [P, CT, HID], F32R)
        wuT = sb("wuT", [P, CT, HID], F32R)
        wdT = sb("wdT", [P, NH, D], F32R)
        bo_rows = sb("bo_rows", [P, D], F32)
        minus_half = sb("minus_half", [P, TT], F32)
        eps_ln = sb("eps_ln", [P, TT], F32)
        zeros = sb("zeros", [P, T], BF16)
        x_in = sb("x_in", [P, TT, D], F32)
        ones = sb("ones", [3, T], BF16)
        parts = sb("parts", [P, 4, 3, T], BF16)
        qs = [sb(f"qs{n}", [KM, H, T], BF16) for n in range(2)]
        ks = [sb(f"ks{n}", [KM, H, T], BF16) for n in range(2)]
        v1 = [sb(f"v1_{n}", [P, TT, H, 2 * DH], F32) for n in range(2)]
        negmax = sb("negmax", [P, 2, 4, TT], F32)
        mrest = sb("mrest", [P, 2, 16], F32)
        mparts = sb("mparts", [P, 2, 64], BF16)
        mrows = sb("mrows", [P, P], BF16)
        e = sb("e", [P, RING, 4, T], F32)
        oT = sb("oT", [P, QUADS, T], F32)
        den = sb("den", [P, 2, H], F32)
        rden = sb("rden", [P, 2, H], F32)
        att = sb("att", [P, TT, D], F32)
        res = sb("res", [P, TT, D], F32)
        stats = sb("stats", [P, 2, TT, 6], F32)
        mv = sb("mv", [P, 2, TT, 2], F32)
        veps = sb("veps", [P, 2, TT], F32)
        rstd = sb("rstd", [P, 2, TT], F32)
        nmean = sb("nmean", [P, 2, TT], F32)
        shift = sb("shift", [P, 2, TT], F32)
        x1h = sb("x1h", [P, CT, T], F32R)
        x1l = sb("x1l", [P, CT, T], F32R)
        xTh, xTl = x1h, x1l
        th = sb("th", [P, 2, T], F32)
        hf = sb("hf", [P, 2, T], F32)
        rest = hf
        hh = sb("hh", [P, NH, T], F32R)
        hl = sb("hl", [P, NH, T], F32R)
        attTh, attTl = hh[:, 0:CT, :], hl[:, 0:CT, :]
        w_stage = oT[:, :, :].rearrange("p q (a c) -> p q a c", a=2)
        i_stage = [e[:, :, :, :].rearrange("p r j t -> p (r j t)")[:, k * 1536:(k + 1) * 1536] for k in range(2)]
        i_stage.append(att[:, :, :].rearrange("p a c -> p (a c)"))

        rm_ps = ctx.enter_context(nc.psum_tensor("rm_ps", [P, 2, T], F32))
        sc_ps = ctx.enter_context(nc.psum_tensor("sc_ps", [P, 2, T], F32))
        pv_ps = ctx.enter_context(nc.psum_tensor("pv_ps", [P, T], F32))
        pr_ps = ctx.enter_context(nc.psum_tensor("pr_ps", [P, T], F32))
        fi_ps = ctx.enter_context(nc.psum_tensor("fi_ps", [P, 2, T], F32))

        w_in = [sem(f"w_in{n}") for n in range(2)]
        w_flt = sem("w_flt")
        ready = sem("ready")
        ready_d = sem("ready_d")
        w_done, wl_done = sem("w_done"), sem("wl_done")
        ones_in = sem("ones_in")
        x_landed = sem("x_landed")
        bo_landed = sem("bo_landed")
        pr_full = sem("pr_full")
        xth_done, xtl_done = sem("xth_done"), sem("xtl_done")
        p1_done, r_done, p2_done, p3_done = sem("p1_done"), sem("r_done"), sem("p2_done"), sem("p3_done")
        stacked = [sem(f"stacked{m}") for m in range(2)]
        v_done = sem("v_done")
        rm_full, rm_free = sem("rm_full"), sem("rm_free")
        m_step, m_split = sem("m_step"), sem("m_split")
        mrow_in = [sem(f"mrow_in{q}") for q in range(QUADS)]
        sc_full, exp_done = sem("sc_full"), sem("exp_done")
        pv_done, ot_done = sem("pv_done"), sem("ot_done")
        fi_full = [sem(f"fi_full{k}") for k in range(2)]
        norm_step, att_done = sem("norm_step"), sem("att_done")
        ath_done, atl_done = sem("ath_done"), sem("atl_done")
        res_landed, res_bo = sem("res_landed"), sem("res_bo")
        r1_done, r2_done = sem("r1_done"), sem("r2_done")
        st_done, mv_done = sem("st_done"), sem("mv_done")
        ve_done, rp_done, rs_done = sem("ve_done"), sem("rp_done"), sem("rs_done")
        x1_done, x1h_done, x1l_done = sem("x1_done"), sem("x1h_done"), sem("x1l_done")
        th_done, pg_done, hf_done, hh_done, hl_done = (
            sem("th_done"), sem("pg_done"), sem("hf_done"), sem("hh_done"), sem("hl_done"))
        y_done, stored = sem("y_done"), sem("stored")

        def fi_tasks(bank, b, k):
            return b * 12 + (W_TASKS + 1 - bank) // 2 + k // 2

        def w_halves(n, half, bank):
            w = (wqT, wkT, wvT, woT)[n][:, half]
            if n >= 2:
                return [(w, bank.rearrange("p (c o) -> p c o", c=CT))]
            return [(w[:, c, :].rearrange("p (m d h) -> p m h d", m=2, h=8),
                     bank[:, c * D:(c + 1) * D].rearrange("p (m h d) -> p m h d", m=2, h=8)) for c in range(CT)]

        def iterations(eng, body):
            def live(i):
                return 0 <= i + 1 < NB, 0 <= i < NB, 0 <= i - 1 < NB
            for i in range(-1, 2):
                body(i, i % 2, live(i), i)
            end = 2 + (NB - 4) // 2 * 2
            with eng.Fori(1, end // 2) as pair:
                body(2 * pair, 0, (True,) * 3, 2)
                body(2 * pair + 1, 1, (True,) * 3, 3)
            for i in range(end, NB + 1):
                body(i, i % 2, live(i), i)

        block = ctx.enter_context(nc.Block())

        @block.sync
        def _(sp):
            sp.dma_start(x_in[:, :, :], x[0].rearrange("(t p) c -> p t c", p=P)).then_inc(x_landed, 16)
            for k, w in enumerate((wq, wk, wv, wo)):
                sp.dma_start(w_stage[:, k], w.rearrange("(a p) c -> p a c", p=P)).then_inc(w_in[0], 16)
            for stage, w in zip(i_stage[:2], (wg, wu)):
                sp.dma_start(stage.bitcast(I32).rearrange("p (a c) -> p a c", c=D),
                             w.rearrange("(a p) c -> p a c", p=P)).then_inc(w_in[1], 16)
            for k in range(2):
                dst = i_stage[2][:, 0:HID] if k == 0 else res[:, :, :].rearrange("p a c -> p (a c)")[:, 0:HID]
                sp.dma_start(dst.bitcast(I32), wd[k * P:(k + 1) * P, :]).then_inc(w_in[1], 16)
            sp.dma_start(bo_rows[:, :], bo.rearrange("(a n) -> a n", a=1).broadcast_to([P, D])).then_inc(bo_landed, 16)
            sp.wait_ge(ready_d, 1)
            for n in range(2):
                sp.dma_start(ks[n][KQ:KM, :, :], ones[:, :].unsqueeze(1).broadcast_to([3, H, T])).then_inc(ones_in, 16)

            def stack(b, par, m):
                sp.wait_ge(p3_done, 4 * b + 2 * m + 2)
                for which, dst, terms in ((0, qs, Q_TERMS), (1, ks, K_TERMS)):
                    for n, part in enumerate(terms):
                        sp.dma_start(dst[par][16 * n:16 * n + 16, 8 * m:8 * m + 8, :], parts[:, 2 * m + which, part, :])\
                          .then_inc(stacked[m], 16)

            def first_stack(m):
                for which, part in ((0, 0), (0, 1), (1, 0), (0, 2), (1, 1), (1, 2)):
                    sp.wait_ge((p1_done, p2_done, p3_done)[part], 2 * m + which + 1)
                    for n, term in enumerate((Q_TERMS, K_TERMS)[which]):
                        if term == part:
                            sp.dma_start((qs, ks)[which][0][16 * n:16 * n + 16, 8 * m:8 * m + 8, :],
                                         parts[:, 2 * m + which, part, :]).then_inc(stacked[m], 16)

            def mrow(b, nb, par, Q):
                tb, at = turn_at(b, nb, Q)
                sp.wait_ge(rm_free, RM_PER * tb + at + 1)
                sp.dma_start(qs[par][KQ:KM, 4 * Q:4 * Q + 4, :], mrows[64 * (Q % 2):64 * (Q % 2) + 48, :])\
                  .then_inc(mrow_in[Q], 16)

            def body(i, par, live, n):
                project, attend, finish = live
                if n + 2 < NB:
                    sp.wait_ge(pr_full, 8 * (i + 1) + CT)
                    sp.dma_start(x_in[:, :, :], x[i + 2].rearrange("(t p) c -> p t c", p=P)).then_inc(x_landed, 16)
                if n >= 2:
                    store(i - 2)
                if finish:
                    if n >= 2:
                        sp.wait_ge(stored, 16 * (i - 1))
                    else:
                        sp.wait_ge(w_done, W_TASKS)
                    sp.dma_start(res[:, :, :], x[i - 1].rearrange("(t p) c -> p t c", p=P)).then_inc(res_landed, 16)
                if attend:
                    mrow(i, n, par, 1)
                if n == -1:
                    first_stack(0)
                    first_stack(1)
                elif project:
                    stack(i + 1, 1 - par, 0)
                if attend:
                    mrow(i, n, par, 2)
                if project and n >= 0:
                    stack(i + 1, 1 - par, 1)
                if attend:
                    mrow(i, n, par, 3)
                if project:
                    mrow(i + 1, n + 1, 1 - par, 0)

            def store(b):
                sp.wait_ge(y_done, b + 1)
                sp.dma_start(out[b].rearrange("(t p) c -> p t c", p=P), res[:, :, :]).then_inc(stored, 16)

            iterations(sp, body)
            store(NB - 1)
            sp.wait_ge(stored, 16 * NB)

        @block.gpsimd
        def _(pool):
            nc.gpsimd.memset(ident[:, :], 0.0).then_inc(ready, 1)
            pool.wait_ge(ready, 1)
            nc.gpsimd.affine_select(out=ident[:, :], in_=ident[:, :], compare_op=ALU.not_equal, fill=1.0,
                                    base=0, pattern=[[-1, P]], channel_multiplier=1).then_inc(ready, 1)
            nc.gpsimd.memset(minus_half[:, :], -0.5)
            nc.gpsimd.memset(eps_ln[:, :], EPS_LN)
            nc.gpsimd.memset(zeros[:, :], 0.0)
            nc.gpsimd.memset(mparts[:, :, :], 0.0).then_inc(ready, 1)
            for n in range(2):
                nc.gpsimd.memset(v1[n][:, :, :, DH:], 1.0).then_inc(ready, 1)

            pool.wait_ge(ready, 5)

            def split(b, m):
                pool.wait_ge(r_done, 4 * b + m + 1)
                nc.gpsimd.tensor_tensor(parts[:, m, 1, :], rest[:, m % 2, :], zeros[:, :], ALU.add).then_inc(p2_done, 1)
                pool.wait_ge(p2_done, 4 * b + m + 1)
                nc.gpsimd.tensor_tensor(parts[:, m, 2, :], rest[:, m % 2, :], parts[:, m, 1, :],
                                        ALU.subtract).then_inc(p3_done, 1)

            def max_parts(b, Q, n):
                k = Q % 2
                step = 3 * (QUADS * b + Q)
                m = negmax[:, k].rearrange("p j t -> p (j t)")
                pool.wait_ge(rm_free, RM_PER * b + rm_at(n, ("tile", 16 * Q + 15)) + 1)
                nc.gpsimd.tensor_tensor(mparts[:, k, 0:16], m, zeros[:, 0:16], ALU.add).then_inc(m_step, 1)
                pool.wait_ge(m_step, step + 1)
                nc.gpsimd.tensor_tensor(mrest[:, k, :], m, mparts[:, k, 0:16], ALU.subtract).then_inc(m_step, 1)
                pool.wait_ge(m_step, step + 2)
                nc.gpsimd.tensor_tensor(mparts[:, k, 16:32], mrest[:, k, :], zeros[:, 0:16], ALU.add).then_inc(m_step, 1)
                pool.wait_ge(m_step, step + 3)
                nc.gpsimd.tensor_tensor(mparts[:, k, 32:48], mrest[:, k, :], mparts[:, k, 16:32],
                                        ALU.subtract).then_inc(m_split, 1)

            def rsqrt(b, k):
                pool.wait_ge(mv_done, 2 * b + k + 1)
                nc.gpsimd.tensor_tensor(nmean[:, k, :], zeros[:, 0:TT], mv[:, k, :, 0], ALU.subtract)
                nc.gpsimd.tensor_tensor(veps[:, k, :], mv[:, k, :, 1], eps_ln[:, :], ALU.add).then_inc(ve_done, 1)
                pool.wait_ge(ve_done, 2 * b + k + 1)
                nc.gpsimd.tensor_tensor(rstd[:, k, :], veps[:, k, :], minus_half[:, :], ALU.pow).then_inc(rp_done, 1)
                pool.wait_ge(rp_done, 2 * b + k + 1)
                nc.gpsimd.tensor_tensor(shift[:, k, :], nmean[:, k, :], rstd[:, k, :], ALU.mult).then_inc(rs_done, 1)

            def body(i, par, live, n):
                project, attend, finish = live
                for s in range(SLOTS):
                    if n >= 2 and s == 3:
                        rsqrt(i - 2, 1)
                    if finish and s == 12:
                        if n == 1:
                            pool.wait_ge(bo_landed, 16)
                        pool.wait_ge(res_landed, 16 * i)
                        for t in range(TT):
                            last = nc.gpsimd.tensor_tensor(res[:, t, :], res[:, t, :], bo_rows[:, :], ALU.add)
                        last.then_inc(res_bo, 1)
                    if finish and s == S_OUT[3] + 3:
                        rsqrt(i - 1, 0)
                    ps = project_slot(n, s)
                    if project and ps - 3 in S_QK2:
                        split(i + 1, S_QK2.index(ps - 3))
                    b, nb, tile = rowmax_of(i, n, s)
                    if tile % 16 == 0:
                        if tile and 0 <= nb < NB:
                            max_parts(b, tile // 16 - 1, nb)
                        elif tile == 0 and 0 < nb <= NB:
                            max_parts(b - 1, QUADS - 1, nb - 1)
                    if finish and s - 4 in S_UP[2::3]:
                        k = S_UP[2::3].index(s - 4)
                        pool.wait_ge(hh_done, NH * (i - 1) + k + 1)
                        nc.gpsimd.tensor_tensor(hl[:, k, :], hf[:, k % 2, :], hh[:, k, :].bitcast(F32),
                                                ALU.subtract).then_inc(hl_done, 1)
            iterations(pool, body)
            rsqrt(NB - 1, 1)

        @block.scalar
        def _(act):
            def copy(dst, src):
                return nc.scalar.activation(dst, src, ACT.Copy)

            def weights(n0, n1):
                for n in range(n0, n1):
                    act.wait_ge(fi_full[n % 2], n // 2 + 1)
                    bank = fi_ps[:, n % 2, :]
                    if n < 4:
                        for dst, src in w_halves(n, 0, bank):
                            last = copy(dst, src)
                        last.then_inc(w_done, 1)
                        continue
                    if n < 10:
                        r = (n - 4) % 3
                        dst = (wgT if n < 7 else wuT)[:, :, 256 * r:256 * r + 256]
                        bank = bank.rearrange("p (c o) -> p c o", c=CT)
                    else:
                        dst = wdT[:, 2 * (n - 10):2 * (n - 10) + 2, :]
                        bank = bank.rearrange("p (a o) -> p a o", a=2)
                    copy(dst, bank).then_inc(w_done, 1)

            def body(i, par, live, n):
                project, attend, finish = live
                for s in range(SLOTS):
                    if n == -1 and s in W_SLOTS:
                        weights(*W_SLOTS[s])
                    ps = project_slot(n, s)
                    if project and ps - 1 in S_XT:
                        k = S_XT.index(ps - 1)
                        act.wait_ge(pr_full, 8 * (i + 1) + k + 1)
                        copy(xTh[:, k, :], pr_ps[:, :]).then_inc(xth_done, 1)
                    if project and ps - 1 in S_QK2:
                        m = S_QK2.index(ps - 1)
                        act.wait_ge(pr_full, 8 * (i + 1) + PR_AT["qk", m] + 1)
                        if n > -1:
                            act.wait_ge(stacked[m // 2], 192 * (i + 1))
                        copy(parts[:, m, 0, :], pr_ps[:, :]).then_inc(p1_done, 1)
                    if project and ps - 1 in S_V[1::2]:
                        k = S_V[1::2].index(ps - 1)
                        act.wait_ge(pr_full, 8 * (i + 1) + PR_AT["v", k] + 1)
                        copy(v1[1 - par][:, 2 * k:2 * k + 2, :, 0:DH],
                             pr_ps[:, :].rearrange("p (t h d) -> p t h d", t=2, h=H)).then_inc(v_done, 1)
                    if attend:
                        j, kt, Q = s % 4, s // 4 % TT, s // 16
                        if j == 0 and (n > 0 or s // 4 >= RING):
                            act.wait_ge(pv_done, 16 * i + s // 4 - RING + 1)
                        act.wait_ge(sc_full, SLOTS * i + s + 1)
                        nc.scalar.activation(e[:, s // 4 % RING, j, :], sc_ps[:, s % 2, :], ACT.Exp, scale=0.25)\
                            .then_inc(exp_done, 1)
                        if s >= 16 + PVLAG and s % 16 == PVLAG:
                            ot_copy(i, s // 16 - 1, n)
                    if n >= 2 and s == 5:
                        normalise(i - 2, 1, y_done)
                    if not finish:
                        continue
                    if s == S_OUT[3] + 5:
                        normalise(i - 1, 0, x1_done)
                    if s == S_BACK[0] + 1:
                        for k in range(CT):
                            act.wait_ge(fi_full[k], fi_tasks(k, i - 1, 4) + 1)
                            copy(attTh[:, k, :], fi_ps[:, k, :]).then_inc(ath_done, 1)
                    if s == S_X1T[0] + 1:
                        for k in range(CT):
                            act.wait_ge(fi_full[k], fi_tasks(k, i - 1, 8) + 1)
                            copy(x1h[:, k, :], fi_ps[:, k, :]).then_inc(x1h_done, 1)
                    if s - 1 in S_UP[1::3]:
                        k = S_UP[1::3].index(s - 1)
                        act.wait_ge(fi_full[0], fi_tasks(0, i - 1, 10 + 2 * k) + 1)
                        if k >= 2 or n > 1:
                            act.wait_ge(hf_done, NH * (i - 1) + k - 1)
                        nc.scalar.activation(th[:, k % 2, :], fi_ps[:, 0, :], ACT.Tanh, scale=0.5 * W_SCALE)\
                            .then_inc(th_done, 1)
                    if s - 3 in S_UP[2::3]:
                        k = S_UP[2::3].index(s - 3)
                        act.wait_ge(hf_done, NH * (i - 1) + k + 1)
                        copy(hh[:, k, :], hf[:, k % 2, :]).then_inc(hh_done, 1)
                if attend:
                    ot_copy(i, QUADS - 1, n)

            def normalise(b, k, done):
                act.wait_ge(rs_done, 2 * b + k + 1)
                for t in range(TT):
                    last = nc.scalar.activation(res[:, t, :], res[:, t, :], ACT.Identity, bias=shift[:, k, t:t + 1],
                                                scale=rstd[:, k, t:t + 1])
                last.then_inc(done, 1)

            def ot_copy(i, Q, n):
                act.wait_ge(pv_done, 16 * i + 4 * Q + 4)
                if Q == 0 and n > 0:
                    act.wait_ge(att_done, TT * i)
                copy(oT[:, Q, :], pv_ps[:, :]).then_inc(ot_done, 1)

            iterations(act, body)
            normalise(NB - 1, 1, y_done)

        @block.vector
        def _(dve):
            nc.vector.memset(ones[:, :], 1.0).then_inc(ready_d, 1)
            dve.wait_ge(ready, 2)
            nc.vector.tensor_copy(identb[:, :], ident[:, :]).then_inc(ready_d, 1)

            def low_weights(n0, n1):
                for n in range(n0, min(n1, 4)):
                    bank = fi_ps[:, n % 2, :]
                    dve.wait_ge(w_done, n + 1)
                    for (low, src), (high, _) in zip(w_halves(n, 1, bank), w_halves(n, 0, bank)):
                        last = nc.vector.tensor_tensor(low, src, high.bitcast(F32), ALU.subtract)
                    last.then_inc(wl_done, 1)

            def low_half(bank, high, low, done):
                nc.vector.tensor_tensor(low, bank, high.bitcast(F32), ALU.subtract).then_inc(done, 1)

            def stats_of(b, k, src, t0):
                for t in (t0, t0 + 1):
                    last = nc.vector.bn_stats(stats[:, k, t, :], src[:, t, :])
                last.then_inc(st_done, 1)

            def mean_var(b, k):
                for t in range(TT):
                    last = nc.vector.bn_aggr(mv[:, k, t, :], stats[:, k, t, :])
                last.then_inc(mv_done, 1)

            def rowmax(b, nb, tile):
                j, t, Q = tile // TT % 4, tile % TT, tile // 16
                if nb < NB:
                    at = rm_at(nb, ("tile", tile))
                    dve.wait_ge(rm_full, RM_PER * b + at + 1)
                    if tile % 16 == 0 and (Q >= 2 or nb > 0):
                        dve.wait_ge(m_split, QUADS * b + Q - 1)
                    nc.vector.tensor_reduce(negmax[:, Q % 2, j, t:t + 1], rm_ps[:, at % 2, :], AX.X, ALU.max,
                                            negate=True).then_inc(rm_free, 1)
                if tile % 16 == MLAG - 1:
                    if Q:
                        m_out(b, nb, Q - 1)
                    elif nb:
                        m_out(b - 1, nb - 1, QUADS - 1)

            def m_out(b, nb, Q):
                tb, at = turn_at(b, nb, Q)
                dve.wait_ge(rm_full, RM_PER * tb + at + 1)
                if Q >= 2 or nb > 0:
                    dve.wait_ge(mrow_in[(Q + 2) % 4], 16 * b + (16 if Q >= 2 else 0))
                r = 64 * (Q % 2)
                nc.vector.tensor_copy(mrows[r:r + 48, :], rm_ps[:, at % 2, :].bitcast(BF16)[r:r + 48, 0:P])\
                    .then_inc(rm_free, 1)

            def body(i, par, live, n):
                project, attend, finish = live
                b = i - 1
                for s in range(SLOTS):
                    if n == -1 and s in W_SLOTS:
                        low_weights(*W_SLOTS[s])
                    if n == -1 and s == S_V[0]:
                        dve.wait_ge(w_in[1], 64)
                        for stage in (i_stage[0], i_stage[1], i_stage[2][:, 0:HID],
                                      res[:, :, :].rearrange("p a c -> p (a c)")[:, 0:HID]):
                            nc.vector.tensor_copy(stage, stage.bitcast(I32)).then_inc(w_flt, 1)
                    if finish and s == S_OUT[3] + 3:
                        dve.wait_ge(st_done, 4 * b + 2)
                    if n >= 2 and s == 2:
                        dve.wait_ge(st_done, 4 * (i - 2) + 4)
                    rb, nb, tile = rowmax_of(i, n, s)
                    if 0 <= nb < NB or (nb == NB and tile == MLAG - 1):
                        rowmax(rb, nb, tile)
                    if n >= 2:
                        norm2(i - 2, s)
                    if finish and s == S_OUT[3] + 3:
                        mean_var(b, 0)
                    ps = project_slot(n, s)
                    if project and ps - 1 in S_XT:
                        k = S_XT.index(ps - 1)
                        dve.wait_ge(xth_done, CT * (i + 1) + k + 1)
                        low_half(pr_ps[:, :], xTh[:, k, :], xTl[:, k, :], xtl_done)
                    if project and ps - 1 in S_QK2:
                        m = S_QK2.index(ps - 1)
                        dve.wait_ge(p1_done, 4 * (i + 1) + m + 1)
                        if m >= 2 or n > -1:
                            dve.wait_ge(p3_done, 4 * (i + 1) + m - 1)
                        nc.vector.tensor_tensor(rest[:, m % 2, :], pr_ps[:, :], parts[:, m, 0, :],
                                                ALU.subtract).then_inc(r_done, 1)
                    if not finish:
                        continue
                    for t in range(TT):
                        if s == S_DIVIDE[t]:
                            attention(b, t, n)
                    if s == S_BACK[0] + 2:
                        for k in range(CT):
                            dve.wait_ge(ath_done, CT * b + k + 1)
                            low_half(fi_ps[:, k, :], attTh[:, k, :], attTl[:, k, :], atl_done)
                    if s - 1 in S_OUT[1::2]:
                        k = S_OUT[1::2].index(s - 1)
                        dve.wait_ge(fi_full[k], fi_tasks(k, b, 6) + 1)
                        if k == 0:
                            dve.wait_ge(res_bo, b + 1)
                        half = res[:, 2 * k:2 * k + 2, :].rearrange("p a c -> p (a c)")
                        nc.vector.tensor_tensor(half, fi_ps[:, k, :], half, ALU.add).then_inc(r1_done, 1)
                    if s - 2 in S_OUT[1::2]:
                        k = S_OUT[1::2].index(s - 2)
                        dve.wait_ge(r1_done, 2 * b + k + 1)
                        stats_of(b, 0, res, 2 * k)
                    if s == S_X1T[0] + 2:
                        for k in range(CT):
                            dve.wait_ge(x1h_done, CT * b + k + 1)
                            low_half(fi_ps[:, k, :], x1h[:, k, :], x1l[:, k, :], x1l_done)
                    if s - 2 in S_UP[1::3]:
                        k = S_UP[1::3].index(s - 2)
                        dve.wait_ge(th_done, NH * b + k + 1)
                        nc.vector.scalar_tensor_tensor(th[:, k % 2, :], th[:, k % 2, :], 1.0, fi_ps[:, 0, :],
                                                       ALU.add, ALU.mult).then_inc(pg_done, 1)
                    if s - 2 in S_UP[2::3]:
                        k = S_UP[2::3].index(s - 2)
                        dve.wait_ge(fi_full[1], fi_tasks(1, b, 11 + 2 * k) + 1)
                        dve.wait_ge(pg_done, NH * b + k + 1)
                        if k == 0 and project:
                            dve.wait_ge(p3_done, 4 * (i + 1) + 4)
                        if k >= 2 or n > 1:
                            dve.wait_ge(hl_done, NH * b + k - 1)
                        nc.vector.tensor_tensor(hf[:, k % 2, :], fi_ps[:, 1, :], th[:, k % 2, :],
                                                ALU.mult).then_inc(hf_done, 1)
                if finish:
                    for k in range(2):
                        down(i, b, k, n)

            def norm2(b, s):
                if s in (0, 1):
                    dve.wait_ge(r2_done, 2 * b + s + 1)
                    stats_of(b, 1, res, 2 * s)
                if s == 2:
                    mean_var(b, 1)

            def attention(b, t, n):
                bank = fi_ps[:, t % 2, :].rearrange("p (h c) -> p h c", c=2 * DH)
                dve.wait_ge(fi_full[t % 2], fi_tasks(t % 2, b, t) + 1)
                nc.vector.tensor_scalar(den[:, t % 2, :], bank[:, :, DH], EPS_DEN, None, ALU.add)\
                    .then_inc(norm_step, 1)
                dve.wait_ge(norm_step, 8 * b + 2 * t + 1)
                nc.vector.reciprocal(rden[:, t % 2, :], den[:, t % 2, :]).then_inc(norm_step, 1)
                dve.wait_ge(norm_step, 8 * b + 2 * t + 2)
                nc.vector.tensor_tensor(att[:, t, :].rearrange("p (h d) -> p h d", d=DH), bank[:, :, 0:DH],
                                        rden[:, t % 2, :].unsqueeze(2).broadcast_to([P, H, DH]),
                                        ALU.mult).then_inc(att_done, 1)

            def down(i, b, k, n):
                dve.wait_ge(fi_full[k], fi_tasks(k, b, 22) + 1)
                nc.vector.scalar_tensor_tensor(
                    res[:, 2 * k:2 * k + 2, :].rearrange("p a c -> p (a c)"), fi_ps[:, k, :], 0.5 * W_SCALE ** 3,
                    res[:, 2 * k:2 * k + 2, :].rearrange("p a c -> p (a c)"), ALU.mult, ALU.add).then_inc(r2_done, 1)

            iterations(dve, body)
            for s in range(3):
                if s == 2:
                    dve.wait_ge(st_done, 4 * NB)
                norm2(NB - 1, s)

        @block.tensor
        def _(pe):
            mm = nc.tensor.matmul

            def weights(n0, n1):
                for n in range(n0, n1):
                    if n >= 2:
                        pe.wait_ge(w_done, n - 1)
                        pe.wait_ge(wl_done, min(n - 1, 4))
                    bank = fi_ps[:, n % 2, :]
                    for c in range(4):
                        if n < 4:
                            src = w_stage[:, n, c % 2, (c // 2) * P:(c // 2 + 1) * P]
                        elif n < 10:
                            r = (n - 4) % 3
                            src = i_stage[(n - 4) // 3].rearrange("p (a c) -> p a c", c=D)[
                                :, 2 * r + c % 2, (c // 2) * P:(c // 2 + 1) * P]
                        else:
                            half = (i_stage[2], res[:, :, :].rearrange("p a c -> p (a c)"))[c % 2]
                            hid = 2 * (n - 10) + c // 2
                            src = half[:, hid * P:(hid + 1) * P]
                        last = nc.tensor.transpose(bank[:, c * P:(c + 1) * P], src, ident[:, :])
                    last.then_inc(fi_full[n % 2], 1)

            def halves(out_, left, right, which):
                steps = [(a, b_, c) for a, b_ in ((1, 0), (0, 1), (0, 0)) for c in range(CT)]
                for k in which:
                    a, b_, c = steps[k]
                    last = mm(out_, left(a, c), right(b_, c), start=(k == 0), stop=(k == 5))
                return last

            def rowmax(b, nb, tile, par):
                j, t, Q = tile // TT % 4, tile % TT, tile // 16
                if nb < NB:
                    at = rm_at(nb, ("tile", tile))
                    if tile % 32 == 0:
                        pe.wait_ge(stacked[tile // 32], 192 * (b + 1))
                    if nb > 0 or at >= 2:
                        pe.wait_ge(rm_free, RM_PER * b + at - 1)
                    h = 4 * Q + j
                    mm(rm_ps[:, at % 2, :], qs[par][0:KQ, h, t * P:(t + 1) * P], ks[par][0:KQ, h, :],
                       start=True, stop=True).then_inc(rm_full, 1)
                if tile % 16 == MLAG - 1:
                    if Q:
                        m_turn(b, nb, Q - 1)
                    elif nb:
                        m_turn(b - 1, nb - 1, QUADS - 1)

            def m_turn(b, nb, Q):
                tb, at = turn_at(b, nb, Q)
                pe.wait_ge(m_split, QUADS * b + Q + 1)
                pe.wait_ge(rm_free, RM_PER * tb + at - 1)
                if nb == 0 and Q == 0:
                    pe.wait_ge(ready_d, 2)
                nc.tensor.transpose(rm_ps[:, at % 2, :].bitcast(BF16)[:, 0:P],
                                    mparts[:, :, :].rearrange("p a m -> p (a m)"), identb[:, :]).then_inc(rm_full, 1)

            def body(i, par, live, n):
                project, attend, finish = live
                b = i - 1
                if n == -1:
                    pe.wait_ge(ready, 2)
                for s in range(SLOTS):
                    if n == -1 and s in W_SLOTS:
                        if W_SLOTS[s][0] == 0:
                            pe.wait_ge(w_in[0], 64)
                        elif W_SLOTS[s][0] == 4:
                            pe.wait_ge(w_flt, 4)
                        weights(*W_SLOTS[s])
                        if W_SLOTS[s][1] <= 4:
                            pe.wait_ge(wl_done, W_SLOTS[s][1])
                    rb, nb, tile = rowmax_of(i, n, s)
                    if 0 <= nb < NB or (nb == NB and tile == MLAG - 1):
                        rowmax(rb, nb, tile, par if nb == n else 1 - par)
                    if attend:
                        j, kt, Q = s % 4, s // 4 % TT, s // 16
                        h = 4 * Q + j
                        if n == 0 and s == 0:
                            pe.wait_ge(ready, 5)
                            pe.wait_ge(ones_in, 32)
                        if s % 16 == 0:
                            pe.wait_ge(mrow_in[Q], 16 * (i + 1))
                        if n > 0 or s >= 2:
                            pe.wait_ge(exp_done, SLOTS * i + s - 1)
                        mm(sc_ps[:, s % 2, :], ks[par][0:KM, h, kt * P:(kt + 1) * P], qs[par][0:KM, h, :],
                           start=True, stop=True).then_inc(sc_full, 1)
                        if s >= 3 + PVLAG and (s - 3 - PVLAG) % 4 == 0:
                            product(i, par, (s - 3 - PVLAG) // 4, n)
                    ps = project_slot(n, s)
                    if project and ps in S_XT:
                        k = S_XT.index(ps)
                        if k == 0:
                            pe.wait_ge(x_landed, 16 * (i + 2))
                            if n > -1:
                                pe.wait_ge(r_done, 4 * (i + 1))
                        else:
                            pe.wait_ge(xtl_done, CT * (i + 1) + k)
                        for t in range(TT):
                            last = nc.tensor.transpose(pr_ps[:, t * P:(t + 1) * P], x_in[:, t, k * P:(k + 1) * P],
                                                       ident[:, :])
                        last.then_inc(pr_full, 1)
                    if project and (ps in S_QK or ps in S_QK2):
                        first = ps in S_QK
                        m = (S_QK if first else S_QK2).index(ps)
                        if first:
                            pr_free(i, ("qk", m))
                        w = (wqT, wkT)[m % 2]
                        last = halves(pr_ps[:, :], lambda a, c: w[:, a, c, (m // 2) * P:(m // 2 + 1) * P],
                                      lambda a, c: (xTh, xTl)[a][:, c, :], range(0, 3) if first else range(3, 6))
                        if not first:
                            last.then_inc(pr_full, 1)
                    if project and ps in S_V:
                        t = S_V.index(ps)
                        if t % 2 == 0:
                            pr_free(i, ("v", t // 2))
                        last = halves(pr_ps[:, (t % 2) * D:(t % 2 + 1) * D],
                                      lambda a, c: (xTh, xTl)[a][:, c, t * P:(t + 1) * P],
                                      lambda a, c: wvT[:, a, c, :], range(6))
                        if t % 2:
                            last.then_inc(pr_full, 1)
                    if not finish:
                        continue
                    for t in range(TT):
                        if s == S_TURN[t]:
                            if t == 0:
                                pe.wait_ge(ot_done, QUADS * i)
                            if t >= 2:
                                pe.wait_ge(att_done, TT * b + t - 1)
                            elif n > 1:
                                pe.wait_ge(r2_done, 2 * (b - 1) + t + 1)
                            elif t == 0:
                                pe.wait_ge(w_done, W_TASKS)
                            for Q in range(QUADS):
                                last = nc.tensor.transpose(fi_ps[:, t % 2, Q * P:(Q + 1) * P],
                                                           oT[:, Q, t * P:(t + 1) * P], ident[:, :])
                            last.then_inc(fi_full[t % 2], 1)
                    for c in range(CT):
                        if s == S_BACK[c]:
                            pe.wait_ge(att_done, TT * b + TT)
                            for t in range(TT):
                                last = nc.tensor.transpose(fi_ps[:, c, t * P:(t + 1) * P], att[:, t, c * P:(c + 1) * P],
                                                           ident[:, :])
                            last.then_inc(fi_full[c], 1)
                    if s in S_OUT:
                        t = S_OUT.index(s)
                        if t == 0:
                            pe.wait_ge(atl_done, CT * b + CT)
                        last = halves(fi_ps[:, t // 2, (t % 2) * D:(t % 2 + 1) * D],
                                      lambda a, c: (attTh, attTl)[a][:, c, t * P:(t + 1) * P],
                                      lambda a, c: woT[:, a, c, :], range(6))
                        if t % 2:
                            last.then_inc(fi_full[t // 2], 1)
                    for c in range(CT):
                        if s == S_X1T[c]:
                            pe.wait_ge(x1_done, b + 1)
                            for t in range(TT):
                                last = nc.tensor.transpose(fi_ps[:, c, t * P:(t + 1) * P], res[:, t, c * P:(c + 1) * P],
                                                           ident[:, :])
                            last.then_inc(fi_full[c], 1)
                    if s in S_UP:
                        k, third = divmod(S_UP.index(s), 3)
                        for q in ((0, 1, 2), (3, 4, 5), (6, 7))[third]:
                            bank, c, a = q // 4, q // 2 % 2, q % 2
                            if k == 0 and q in (0, 2):
                                pe.wait_ge(x1l_done, CT * b + c + 1)
                            if q % 4 == 0:
                                if k:
                                    pe.wait_ge((pg_done, hf_done)[bank], NH * b + k)
                            last = mm(fi_ps[:, bank, :], (wgT, wuT)[bank][:, c, k * P:(k + 1) * P],
                                      (x1h, x1l)[a][:, c, :], start=(q % 4 == 0), stop=(q % 4 == 3))
                            if q % 4 == 3:
                                last.then_inc(fi_full[bank], 1)
                    for q in range(len(S_DOWN)):
                        if s == S_DOWN[q]:
                            down(i, q // 5, q % 5)
                if finish:
                    down(i, 0, NH - 1)
                if attend:
                    product(i, par, 15, n)
                if finish:
                    down(i, 1, NH - 1)

            def pr_free(i, key):
                before = {at: k for k, at in PR_AT.items()}[PR_AT[key] - 1]
                if before[0] == "xt":
                    pe.wait_ge(xtl_done, CT * (i + 1) + CT)
                elif before[0] == "qk":
                    pe.wait_ge(r_done, 4 * (i + 1) + before[1] + 1)
                else:
                    pe.wait_ge(v_done, 2 * (i + 1) + before[1] + 1)

            def down(i, k, g):
                b = i - 1
                if g == 0:
                    pe.wait_ge((pg_done, hf_done)[k], NH * b + NH)
                if k == 0:
                    pe.wait_ge(hl_done, NH * b + g + 1)
                for t in (2 * k, 2 * k + 1):
                    for part in (hl, hh):
                        last = mm(fi_ps[:, k, (t % 2) * D:(t % 2 + 1) * D], part[:, g, t * P:(t + 1) * P],
                                  wdT[:, g, :], start=(g == 0 and t % 2 == 0 and part is hl),
                                  stop=(g == NH - 1 and t % 2 == 1 and part is hh), skip_group_check=True)
                if g == NH - 1:
                    last.then_inc(fi_full[k], 1)

            def product(i, par, g, n):
                Q, kt = g // TT, g % TT
                if g == 0:
                    pe.wait_ge(v_done, 2 * (i + 1))
                if kt == 0 and (Q or n > 0):
                    pe.wait_ge(ot_done, QUADS * i + Q)
                pe.wait_ge(exp_done, SLOTS * i + 4 * g + 4)
                for j in range(4):
                    last = mm(pv_ps[32 * j:32 * j + 32, :], v1[par][:, kt, 4 * Q + j, :], e[:, g % RING, j, :],
                              start=(kt == 0), stop=(kt == TT - 1), tile_position=(0, 32 * j))
                last.then_inc(pv_done, 1)

            iterations(pe, body)


_INS = ["L0_attn_x", "L0_attn_Wq", "L0_attn_Wk", "L0_attn_Wv", "L0_attn_Wo", "L0_attn_bo",
        "L0_ffn_w_gate", "L0_ffn_w_up", "L0_ffn_w_down"]


def kernel(**inputs):
    import numpy as _np
    import concourse.bacc as _bacc
    from concourse import mybir as _mybir
    from concourse.bass_utils import run_bass_kernel_spmd as _run

    nc = _bacc.Bacc("TRN2", target_bir_lowering=False, num_devices=1)
    arrays, args = {}, []
    for name in _INS:
        a = _np.ascontiguousarray(inputs[name])
        arrays[f"in_{name}_dram"] = a
        args.append(nc.dram_tensor(f"in_{name}_dram", a.shape, _mybir.dt.from_np(a.dtype), kind="ExternalInput").ap())
    out = nc.dram_tensor("out_0_dram", (NB, T, D), _mybir.dt.float32, kind="ExternalOutput").ap()
    layer_program(nc, *args, out)
    r = _run(nc, [arrays], core_ids=[0])
    return r.results[0]["out_0_dram"]
```

```python
from contextlib import ExitStack

import concourse.bass as bass
from concourse import mybir

F32 = mybir.dt.float32
F32R = mybir.dt.float32r
BF16 = mybir.dt.bfloat16
I32 = mybir.dt.int32
ACT = mybir.ActivationFunctionType
ALU = mybir.AluOpType
AX = mybir.AxisListType

P = 128
NB, T, D = 8, 512, 256
H, DH = 16, 16
HID = 768
TT = T // P
CT = D // P
NH = HID // P
QUADS = H // 4
SLOTS = H * TT
Q_TERMS = (0, 0, 0, 1, 1, 2)
K_TERMS = (0, 1, 2, 0, 1, 0)
KQ = 16 * len(Q_TERMS)
KM = KQ + 3
RING = 2
EPS_DEN = 1e-8
EPS_LN = 1e-5
W_SCALE = 1.0 / 127.0

LEAD = 26
PVLAG = 3
MLAG = 6

S_XT = (0, 3)
S_QK = (7, 11, 19, 26)
S_QK2 = (8, 12, 20, 27)
S_V = (15, 16, 23, 24)
S_TURN = (1, 1, 5, 5)
S_DIVIDE = (2, 3, 6, 7)
S_BIAS = 5
S_STATS2 = (4, 8)
S_MEAN2 = 10
S_NORM2 = (14, 15)
S_NORM = (23, 25)
S_BACK = (9, 9)
S_OUT = (13, 15, 16, 17)
S_X1T = (28, 28)
FREE = [_s for _s in range(31, SLOTS) if _s % 4 != 2]
S_UP = FREE[0:18]
S_DOWN = (FREE[18], FREE[18], FREE[19], FREE[19], FREE[20],
          FREE[21], FREE[21], FREE[22], FREE[22], FREE[23])

PR_AT = {("xt", 0): 0, ("xt", 1): 1}
for _s, _key in sorted([(S_QK2[m], ("qk", m)) for m in range(4)] + [(S_V[2 * k + 1], ("v", k)) for k in range(2)]):
    PR_AT[_key] = len(PR_AT)

RM_ORDER = []
for _s in range(SLOTS):
    RM_ORDER.append(("tile", _s))
    if _s % 16 == MLAG - 1:
        RM_ORDER.append(("turn", (_s // 16 - 1) % QUADS))
RM_AT = {key: n for n, key in enumerate(RM_ORDER)}
RM_PER = len(RM_ORDER)


def rm_at(nb, key):
    if nb == NB:
        return -1
    return RM_AT[key] - (nb > 0 or RM_AT[key] > MLAG)


def turn_at(b, nb, Q):
    if Q < QUADS - 1:
        return b, rm_at(nb, ("turn", Q))
    return b + 1, rm_at(nb + 1, ("turn", Q))


def project_slot(n, s):
    if n >= 0 or s < S_V[0]:
        return s
    return s - (SLOTS - LEAD - 6 - S_V[0]) if s >= SLOTS - LEAD - 6 else -9


def rowmax_of(i, n, s):
    ahead, tile = divmod(s + LEAD, SLOTS)
    return i + ahead, n + ahead, tile


W_TASKS = 4 + 3 * 3
W_SLOTS = {5: (0, 2), 13: (2, 4)}
W_SLOTS.update({SLOTS - LEAD + 3 + _n: (4 + _n, 5 + _n) for _n in range(W_TASKS - 4)})


def layer_program(nc, x, wq, wk, wv, wo, bo, wg, wu, wd, out):
    with ExitStack() as ctx:
        def sb(name, shape, dt):
            return ctx.enter_context(nc.sbuf_tensor(name, shape, dt))

        def sem(name):
            return ctx.enter_context(nc.semaphore(name))

        ident = sb("ident", [P, P], F32)
        identb = sb("identb", [P, P], BF16)
        wqT, wkT, wvT, woT = (sb(n, [P, 2, CT, D], F32R) for n in ("wqT", "wkT", "wvT", "woT"))
        wgT = sb("wgT", [P, CT, HID], F32R)
        wuT = sb("wuT", [P, CT, HID], F32R)
        wdT = sb("wdT", [P, NH, D], F32R)
        bo_rows = sb("bo_rows", [P, D], F32)
        minus_half = sb("minus_half", [P, TT], F32)
        eps_ln = sb("eps_ln", [P, TT], F32)
        zeros = sb("zeros", [P, T], BF16)
        x_in = sb("x_in", [P, TT, D], F32)
        ones = sb("ones", [3, T], BF16)
        parts = sb("parts", [P, 4, 3, T], BF16)
        qs = [sb(f"qs{n}", [KM, H, T], BF16) for n in range(2)]
        ks = [sb(f"ks{n}", [KM, H, T], BF16) for n in range(2)]
        v1 = [sb(f"v1_{n}", [P, TT, H, 2 * DH], F32) for n in range(2)]
        negmax = sb("negmax", [P, 2, 4, TT], F32)
        mrest = sb("mrest", [P, 2, 16], F32)
        mparts = sb("mparts", [P, 2, 64], BF16)
        mrows = sb("mrows", [P, P], BF16)
        e = sb("e", [P, RING, 4, T], F32)
        oT = sb("oT", [P, QUADS, T], F32)
        den = sb("den", [P, 2, H], F32)
        rden = sb("rden", [P, 2, H], F32)
        att = sb("att", [P, TT, D], F32)
        res = sb("res", [P, TT, D], F32)
        stats = sb("stats", [P, 2, TT, 6], F32)
        mv = sb("mv", [P, 2, TT, 2], F32)
        veps = sb("veps", [P, 2, TT], F32)
        rstd = sb("rstd", [P, 2, TT], F32)
        nmean = sb("nmean", [P, 2, TT], F32)
        shift = sb("shift", [P, 2, TT], F32)
        x1h = sb("x1h", [P, CT, T], F32R)
        x1l = sb("x1l", [P, CT, T], F32R)
        xTh, xTl = x1h, x1l
        th = sb("th", [P, 2, T], F32)
        xb = th[:, :, :].rearrange("p k (a c) -> p (k a) c", c=D)
        hf = sb("hf", [P, 2, T], F32)
        rest = hf
        hh = sb("hh", [P, NH, T], F32R)
        hl = sb("hl", [P, NH, T], F32R)
        attTh, attTl = hh[:, 0:CT, :], hl[:, 0:CT, :]
        w_stage = oT[:, :, :].rearrange("p q (a c) -> p q a c", a=2)
        i_stage = [e[:, :, :, :].rearrange("p r j t -> p (r j t)")[:, k * 1536:(k + 1) * 1536] for k in range(2)]
        i_stage.append(att[:, :, :].rearrange("p a c -> p (a c)"))

        rm_ps = ctx.enter_context(nc.psum_tensor("rm_ps", [P, 2, T], F32))
        sc_ps = ctx.enter_context(nc.psum_tensor("sc_ps", [P, 2, T], F32))
        pv_ps = ctx.enter_context(nc.psum_tensor("pv_ps", [P, T], F32))
        pr_ps = ctx.enter_context(nc.psum_tensor("pr_ps", [P, T], F32))
        fi_ps = ctx.enter_context(nc.psum_tensor("fi_ps", [P, 2, T], F32))

        w_in = [sem(f"w_in{n}") for n in range(2)]
        w_flt = sem("w_flt")
        ready = sem("ready")
        ready_d = sem("ready_d")
        w_done, wl_done = sem("w_done"), sem("wl_done")
        ones_in = sem("ones_in")
        x_landed = sem("x_landed")
        bo_landed = sem("bo_landed")
        pr_full = sem("pr_full")
        xth_done, xtl_done = sem("xth_done"), sem("xtl_done")
        p1_done, r_done, p2_done, p3_done = sem("p1_done"), sem("r_done"), sem("p2_done"), sem("p3_done")
        stacked = [sem(f"stacked{m}") for m in range(2)]
        v_done = sem("v_done")
        rm_full, rm_free = sem("rm_full"), sem("rm_free")
        m_step, m_split = sem("m_step"), sem("m_split")
        mrow_in = [sem(f"mrow_in{q}") for q in range(QUADS)]
        sc_full, exp_done = sem("sc_full"), sem("exp_done")
        pv_done, ot_done = sem("pv_done"), sem("ot_done")
        fi_full = [sem(f"fi_full{k}") for k in range(2)]
        norm_step, att_done = sem("norm_step"), sem("att_done")
        ath_done, atl_done = sem("ath_done"), sem("atl_done")
        xb_landed, xb_done = sem("xb_landed"), sem("xb_done")
        r1_done, r2_done = sem("r1_done"), sem("r2_done")
        st_done, mv_done = sem("st_done"), sem("mv_done")
        ve_done, rp_done, rs_done = sem("ve_done"), sem("rp_done"), sem("rs_done")
        x1_done, x1h_done, x1l_done = sem("x1_done"), sem("x1h_done"), sem("x1l_done")
        th_done, pg_done, hf_done, hh_done, hl_done = (
            sem("th_done"), sem("pg_done"), sem("hf_done"), sem("hh_done"), sem("hl_done"))
        y_done, stored = sem("y_done"), sem("stored")

        def fi_tasks(bank, b, k):
            return b * 12 + (W_TASKS + 1 - bank) // 2 + k // 2

        def turn_banks(n, pair):
            return rm_ps if n == NB and pair else fi_ps

        def up_bank(n, k, up):
            return (rm_ps if n == NB and k % 2 else fi_ps)[:, up, :]

        def down_bank(n, k):
            return (sc_ps if n == NB else fi_ps)[:, k, :]

        def w_halves(n, half, bank):
            w = (wqT, wkT, wvT, woT)[n][:, half]
            if n >= 2:
                return [(w, bank.rearrange("p (c o) -> p c o", c=CT))]
            return [(w[:, c, :].rearrange("p (m d h) -> p m h d", m=2, h=8),
                     bank[:, c * D:(c + 1) * D].rearrange("p (m h d) -> p m h d", m=2, h=8)) for c in range(CT)]

        def iterations(eng, body):
            def live(i):
                return 0 <= i + 1 < NB, 0 <= i < NB, 0 <= i - 1 < NB
            for i in range(-1, 2):
                body(i, i % 2, live(i), i)
            end = 2 + (NB - 4) // 2 * 2
            with eng.Fori(1, end // 2) as pair:
                body(2 * pair, 0, (True,) * 3, 2)
                body(2 * pair + 1, 1, (True,) * 3, 3)
            for i in range(end, NB + 1):
                body(i, i % 2, live(i), i)

        block = ctx.enter_context(nc.Block())

        @block.sync
        def _(sp):
            sp.dma_start(x_in[:, :, :], x[0].rearrange("(t p) c -> p t c", p=P)).then_inc(x_landed, 16)
            for k, w in enumerate((wq, wk, wv, wo)):
                sp.dma_start(w_stage[:, k], w.rearrange("(a p) c -> p a c", p=P)).then_inc(w_in[0], 16)
            for stage, w in zip(i_stage[:2], (wg, wu)):
                sp.dma_start(stage.bitcast(I32).rearrange("p (a c) -> p a c", c=D),
                             w.rearrange("(a p) c -> p a c", p=P)).then_inc(w_in[1], 16)
            for k in range(2):
                dst = i_stage[2][:, 0:HID] if k == 0 else res[:, :, :].rearrange("p a c -> p (a c)")[:, 0:HID]
                sp.dma_start(dst.bitcast(I32), wd[k * P:(k + 1) * P, :]).then_inc(w_in[1], 16)
            sp.dma_start(bo_rows[:, :], bo.rearrange("(a n) -> a n", a=1).broadcast_to([P, D])).then_inc(bo_landed, 16)
            sp.wait_ge(ready_d, 1)
            for n in range(2):
                sp.dma_start(ks[n][KQ:KM, :, :], ones[:, :].unsqueeze(1).broadcast_to([3, H, T])).then_inc(ones_in, 16)

            def stack(b, par, m):
                sp.wait_ge(p3_done, 4 * b + 2 * m + 2)
                for which, dst, terms in ((0, qs, Q_TERMS), (1, ks, K_TERMS)):
                    for n, part in enumerate(terms):
                        sp.dma_start(dst[par][16 * n:16 * n + 16, 8 * m:8 * m + 8, :], parts[:, 2 * m + which, part, :])\
                          .then_inc(stacked[m], 16)

            def first_stack(m):
                for which, part in ((0, 0), (0, 1), (1, 0), (0, 2), (1, 1), (1, 2)):
                    sp.wait_ge((p1_done, p2_done, p3_done)[part], 2 * m + which + 1)
                    for n, term in enumerate((Q_TERMS, K_TERMS)[which]):
                        if term == part:
                            sp.dma_start((qs, ks)[which][0][16 * n:16 * n + 16, 8 * m:8 * m + 8, :],
                                         parts[:, 2 * m + which, part, :]).then_inc(stacked[m], 16)

            def mrow(b, nb, par, Q):
                tb, at = turn_at(b, nb, Q)
                sp.wait_ge(rm_free, RM_PER * tb + at + 1)
                sp.dma_start(qs[par][KQ:KM, 4 * Q:4 * Q + 4, :], mrows[64 * (Q % 2):64 * (Q % 2) + 48, :])\
                  .then_inc(mrow_in[Q], 16)

            def body(i, par, live, n):
                project, attend, finish = live
                if finish:
                    if n >= 2:
                        sp.wait_ge(hf_done, NH * (i - 1))
                    sp.dma_start(xb[:, :, :], x[i - 1].rearrange("(t p) c -> p t c", p=P)).then_inc(xb_landed, 16)
                if n + 2 < NB:
                    sp.wait_ge(pr_full, 8 * (i + 1) + CT)
                    sp.dma_start(x_in[:, :, :], x[i + 2].rearrange("(t p) c -> p t c", p=P)).then_inc(x_landed, 16)
                if attend:
                    mrow(i, n, par, 1)
                if n >= 2:
                    store(i - 2)
                if n == -1:
                    first_stack(0)
                    first_stack(1)
                elif project:
                    stack(i + 1, 1 - par, 0)
                if attend:
                    mrow(i, n, par, 2)
                if project and n >= 0:
                    stack(i + 1, 1 - par, 1)
                if attend:
                    mrow(i, n, par, 3)
                if project:
                    mrow(i + 1, n + 1, 1 - par, 0)

            def store(b):
                for k in range(2):
                    sp.wait_ge(y_done, 2 * b + k + 1)
                    sp.dma_start(out[b, 2 * P * k:2 * P * (k + 1)].rearrange("(t p) c -> p t c", p=P), att[:, 2 * k:2 * k + 2, :])\
                      .then_inc(stored, 16)

            iterations(sp, body)
            store(NB - 1)
            sp.wait_ge(stored, 32 * NB)

        @block.gpsimd
        def _(pool):
            nc.gpsimd.memset(ident[:, :], 0.0).then_inc(ready, 1)
            pool.wait_ge(ready, 1)
            nc.gpsimd.affine_select(out=ident[:, :], in_=ident[:, :], compare_op=ALU.not_equal, fill=1.0,
                                    base=0, pattern=[[-1, P]], channel_multiplier=1).then_inc(ready, 1)
            nc.gpsimd.memset(minus_half[:, :], -0.5)
            nc.gpsimd.memset(eps_ln[:, :], EPS_LN)
            nc.gpsimd.memset(zeros[:, :], 0.0)
            nc.gpsimd.memset(mparts[:, :, :], 0.0).then_inc(ready, 1)
            for n in range(2):
                nc.gpsimd.memset(v1[n][:, :, :, DH:], 1.0).then_inc(ready, 1)

            pool.wait_ge(ready, 5)

            def split(b, m):
                pool.wait_ge(r_done, 4 * b + m + 1)
                nc.gpsimd.tensor_tensor(parts[:, m, 1, :], rest[:, m % 2, :], zeros[:, :], ALU.add).then_inc(p2_done, 1)
                pool.wait_ge(p2_done, 4 * b + m + 1)
                nc.gpsimd.tensor_tensor(parts[:, m, 2, :], rest[:, m % 2, :], parts[:, m, 1, :],
                                        ALU.subtract).then_inc(p3_done, 1)

            def max_parts(b, Q, n):
                k = Q % 2
                step = 3 * (QUADS * b + Q)
                m = negmax[:, k].rearrange("p j t -> p (j t)")
                pool.wait_ge(rm_free, RM_PER * b + rm_at(n, ("tile", 16 * Q + 15)) + 1)
                nc.gpsimd.tensor_tensor(mparts[:, k, 0:16], m, zeros[:, 0:16], ALU.add).then_inc(m_step, 1)
                pool.wait_ge(m_step, step + 1)
                nc.gpsimd.tensor_tensor(mrest[:, k, :], m, mparts[:, k, 0:16], ALU.subtract).then_inc(m_step, 1)
                pool.wait_ge(m_step, step + 2)
                nc.gpsimd.tensor_tensor(mparts[:, k, 16:32], mrest[:, k, :], zeros[:, 0:16], ALU.add).then_inc(m_step, 1)
                pool.wait_ge(m_step, step + 3)
                nc.gpsimd.tensor_tensor(mparts[:, k, 32:48], mrest[:, k, :], mparts[:, k, 16:32],
                                        ALU.subtract).then_inc(m_split, 1)

            def rsqrt(b, k):
                pool.wait_ge(mv_done, 2 * b + k + 1)
                nc.gpsimd.tensor_tensor(nmean[:, k, :], zeros[:, 0:TT], mv[:, k, :, 0], ALU.subtract)
                nc.gpsimd.tensor_tensor(veps[:, k, :], mv[:, k, :, 1], eps_ln[:, :], ALU.add).then_inc(ve_done, 1)
                pool.wait_ge(ve_done, 2 * b + k + 1)
                nc.gpsimd.tensor_tensor(rstd[:, k, :], veps[:, k, :], minus_half[:, :], ALU.pow).then_inc(rp_done, 1)
                pool.wait_ge(rp_done, 2 * b + k + 1)
                nc.gpsimd.tensor_tensor(shift[:, k, :], nmean[:, k, :], rstd[:, k, :], ALU.mult).then_inc(rs_done, 1)

            def body(i, par, live, n):
                project, attend, finish = live
                for s in range(SLOTS):
                    if n >= 2 and s == S_MEAN2:
                        rsqrt(i - 2, 1)
                    if finish and s == S_BIAS:
                        if n == 1:
                            pool.wait_ge(bo_landed, 16)
                        pool.wait_ge(xb_landed, 16 * i)
                        for t in range(TT):
                            last = nc.gpsimd.tensor_tensor(xb[:, t, :], xb[:, t, :], bo_rows[:, :], ALU.add)
                        last.then_inc(xb_done, 1)
                    if finish and s == S_OUT[3] + 3:
                        rsqrt(i - 1, 0)
                    ps = project_slot(n, s)
                    if project and ps - 3 in S_QK2:
                        split(i + 1, S_QK2.index(ps - 3))
                    b, nb, tile = rowmax_of(i, n, s)
                    if tile % 16 == 0:
                        if tile and 0 <= nb < NB:
                            max_parts(b, tile // 16 - 1, nb)
                        elif tile == 0 and 0 < nb <= NB:
                            max_parts(b - 1, QUADS - 1, nb - 1)
                    if finish and s - 4 in S_UP[2::3] and (n < NB or s - 4 < S_UP[-1]):
                        k = S_UP[2::3].index(s - 4)
                        pool.wait_ge(hh_done, NH * (i - 1) + k + 1)
                        nc.gpsimd.tensor_tensor(hl[:, k, :], hf[:, k % 2, :], hh[:, k, :].bitcast(F32),
                                                ALU.subtract).then_inc(hl_done, 1)
            iterations(pool, body)
            rsqrt(NB - 1, 1)

        @block.scalar
        def _(act):
            def copy(dst, src):
                return nc.scalar.activation(dst, src, ACT.Copy)

            def weights(n0, n1):
                for n in range(n0, n1):
                    act.wait_ge(fi_full[n % 2], n // 2 + 1)
                    bank = fi_ps[:, n % 2, :]
                    if n < 4:
                        for dst, src in w_halves(n, 0, bank):
                            last = copy(dst, src)
                        last.then_inc(w_done, 1)
                        continue
                    if n < 10:
                        r = (n - 4) % 3
                        dst = (wgT if n < 7 else wuT)[:, :, 256 * r:256 * r + 256]
                        bank = bank.rearrange("p (c o) -> p c o", c=CT)
                    else:
                        dst = wdT[:, 2 * (n - 10):2 * (n - 10) + 2, :]
                        bank = bank.rearrange("p (a o) -> p a o", a=2)
                    copy(dst, bank).then_inc(w_done, 1)

            def body(i, par, live, n):
                project, attend, finish = live
                for s in range(SLOTS):
                    if n == -1 and s in W_SLOTS:
                        weights(*W_SLOTS[s])
                    ps = project_slot(n, s)
                    if project and ps - 1 in S_XT:
                        k = S_XT.index(ps - 1)
                        act.wait_ge(pr_full, 8 * (i + 1) + k + 1)
                        copy(xTh[:, k, :], pr_ps[:, :]).then_inc(xth_done, 1)
                    if project and ps - 1 in S_QK2:
                        m = S_QK2.index(ps - 1)
                        act.wait_ge(pr_full, 8 * (i + 1) + PR_AT["qk", m] + 1)
                        if n > -1:
                            act.wait_ge(stacked[m // 2], 192 * (i + 1))
                        copy(parts[:, m, 0, :], pr_ps[:, :]).then_inc(p1_done, 1)
                    if project and ps - 1 in S_V[1::2]:
                        k = S_V[1::2].index(ps - 1)
                        act.wait_ge(pr_full, 8 * (i + 1) + PR_AT["v", k] + 1)
                        copy(v1[1 - par][:, 2 * k:2 * k + 2, :, 0:DH],
                             pr_ps[:, :].rearrange("p (t h d) -> p t h d", t=2, h=H)).then_inc(v_done, 1)
                    if attend:
                        j, kt, Q = s % 4, s // 4 % TT, s // 16
                        if j == 0 and (n > 0 or s // 4 >= RING):
                            act.wait_ge(pv_done, 16 * i + s // 4 - RING + 1)
                        act.wait_ge(sc_full, SLOTS * i + s + 1)
                        nc.scalar.activation(e[:, s // 4 % RING, j, :], sc_ps[:, s % 2, :], ACT.Exp, scale=0.25)\
                            .then_inc(exp_done, 1)
                        if s >= 16 + PVLAG and s % 16 == PVLAG:
                            ot_copy(i, s // 16 - 1, n)
                    if n >= 2 and s in S_NORM2:
                        normalise(i - 2, 1, S_NORM2.index(s), att, y_done)
                    if not finish:
                        continue
                    if s in S_NORM and n < NB:
                        normalise(i - 1, 0, S_NORM.index(s), res, x1_done)
                    for k in range(CT):
                        if s == S_BACK[k] + 1:
                            act.wait_ge(fi_full[k], fi_tasks(k, i - 1, 4) + 1)
                            copy(attTh[:, k, :], fi_ps[:, k, :]).then_inc(ath_done, 1)
                    for k in range(CT):
                        if s == S_X1T[k] + 1:
                            act.wait_ge(fi_full[k], fi_tasks(k, i - 1, 8) + 1)
                            copy(x1h[:, k, :], fi_ps[:, k, :]).then_inc(x1h_done, 1)
                    if s - 1 in S_UP[1::3]:
                        k = S_UP[1::3].index(s - 1)
                        act.wait_ge(fi_full[0], fi_tasks(0, i - 1, 10 + 2 * k) + 1)
                        if k >= 2 or n > 1:
                            act.wait_ge(hf_done, NH * (i - 1) + k - 1)
                        nc.scalar.activation(th[:, k % 2, :], up_bank(n, k, 0), ACT.Tanh, scale=0.5 * W_SCALE)\
                            .then_inc(th_done, 1)
                    if s - 3 in S_UP[2::3]:
                        k = S_UP[2::3].index(s - 3)
                        act.wait_ge(hf_done, NH * (i - 1) + k + 1)
                        copy(hh[:, k, :], hf[:, k % 2, :]).then_inc(hh_done, 1)
                if attend:
                    ot_copy(i, QUADS - 1, n)

            def normalise(b, k, half, dst, done):
                act.wait_ge(rs_done, 2 * b + k + 1)
                for t in (2 * half, 2 * half + 1):
                    last = nc.scalar.activation(dst[:, t, :], res[:, t, :], ACT.Identity, bias=shift[:, k, t:t + 1],
                                                scale=rstd[:, k, t:t + 1])
                last.then_inc(done, 1)

            def ot_copy(i, Q, n):
                act.wait_ge(pv_done, 16 * i + 4 * Q + 4)
                if Q == 0 and n > 0:
                    act.wait_ge(att_done, TT * i)
                copy(oT[:, Q, :], pv_ps[:, :]).then_inc(ot_done, 1)

            iterations(act, body)

        @block.vector
        def _(dve):
            nc.vector.memset(ones[:, :], 1.0).then_inc(ready_d, 1)
            dve.wait_ge(ready, 2)
            nc.vector.tensor_copy(identb[:, :], ident[:, :]).then_inc(ready_d, 1)

            def low_weights(n0, n1):
                for n in range(n0, min(n1, 4)):
                    bank = fi_ps[:, n % 2, :]
                    dve.wait_ge(w_done, n + 1)
                    for (low, src), (high, _) in zip(w_halves(n, 1, bank), w_halves(n, 0, bank)):
                        last = nc.vector.tensor_tensor(low, src, high.bitcast(F32), ALU.subtract)
                    last.then_inc(wl_done, 1)

            def low_half(bank, high, low, done):
                nc.vector.tensor_tensor(low, bank, high.bitcast(F32), ALU.subtract).then_inc(done, 1)

            def stats_of(b, k, src, t0):
                for t in (t0, t0 + 1):
                    last = nc.vector.bn_stats(stats[:, k, t, :], src[:, t, :])
                last.then_inc(st_done, 1)

            def mean_var(b, k):
                for t in range(TT):
                    last = nc.vector.bn_aggr(mv[:, k, t, :], stats[:, k, t, :])
                last.then_inc(mv_done, 1)

            def last_norm(k, half, dst, done):
                dve.wait_ge(rp_done, 2 * NB - 1 + k)
                for t in (2 * half, 2 * half + 1):
                    last = nc.vector.tensor_scalar(dst[:, t, :], res[:, t, :], mv[:, k, t, 0:1], rstd[:, k, t:t + 1],
                                                   ALU.subtract, ALU.mult)
                last.then_inc(done, 1)

            def rowmax(b, nb, tile):
                j, t, Q = tile // TT % 4, tile % TT, tile // 16
                if nb < NB:
                    at = rm_at(nb, ("tile", tile))
                    dve.wait_ge(rm_full, RM_PER * b + at + 1)
                    if tile % 16 == 0 and (Q >= 2 or nb > 0):
                        dve.wait_ge(m_split, QUADS * b + Q - 1)
                    nc.vector.tensor_reduce(negmax[:, Q % 2, j, t:t + 1], rm_ps[:, at % 2, :], AX.X, ALU.max,
                                            negate=True).then_inc(rm_free, 1)
                if tile % 16 == MLAG - 1:
                    if Q:
                        m_out(b, nb, Q - 1)
                    elif nb:
                        m_out(b - 1, nb - 1, QUADS - 1)

            def m_out(b, nb, Q):
                tb, at = turn_at(b, nb, Q)
                dve.wait_ge(rm_full, RM_PER * tb + at + 1)
                if Q >= 2 or nb > 0:
                    dve.wait_ge(mrow_in[(Q + 2) % 4], 16 * b + (16 if Q >= 2 else 0))
                r = 64 * (Q % 2)
                nc.vector.tensor_copy(mrows[r:r + 48, :], rm_ps[:, at % 2, :].bitcast(BF16)[r:r + 48, 0:P])\
                    .then_inc(rm_free, 1)

            def body(i, par, live, n):
                project, attend, finish = live
                b = i - 1
                for s in range(SLOTS):
                    if n == -1 and s in W_SLOTS:
                        low_weights(*W_SLOTS[s])
                    if n == -1 and s == S_V[0]:
                        dve.wait_ge(w_in[1], 64)
                        for stage in (i_stage[0], i_stage[1], i_stage[2][:, 0:HID],
                                      res[:, :, :].rearrange("p a c -> p (a c)")[:, 0:HID]):
                            nc.vector.tensor_copy(stage, stage.bitcast(I32)).then_inc(w_flt, 1)
                    if finish and s == S_OUT[3] + 3:
                        dve.wait_ge(st_done, 4 * b + 2)
                    if n >= 2 and s == S_MEAN2:
                        dve.wait_ge(st_done, 4 * (i - 2) + 4)
                    rb, nb, tile = rowmax_of(i, n, s)
                    if 0 <= nb < NB or (nb == NB and tile == MLAG - 1):
                        rowmax(rb, nb, tile)
                    if n >= 2:
                        norm2(i - 2, s)
                    if finish and s == S_OUT[3] + 3:
                        mean_var(b, 0)
                    ps = project_slot(n, s)
                    if project and ps - 1 in S_XT:
                        k = S_XT.index(ps - 1)
                        dve.wait_ge(xth_done, CT * (i + 1) + k + 1)
                        low_half(pr_ps[:, :], xTh[:, k, :], xTl[:, k, :], xtl_done)
                    if project and ps - 1 in S_QK2:
                        m = S_QK2.index(ps - 1)
                        dve.wait_ge(p1_done, 4 * (i + 1) + m + 1)
                        if m >= 2 or n > -1:
                            dve.wait_ge(p3_done, 4 * (i + 1) + m - 1)
                        nc.vector.tensor_tensor(rest[:, m % 2, :], pr_ps[:, :], parts[:, m, 0, :],
                                                ALU.subtract).then_inc(r_done, 1)
                    if not finish:
                        continue
                    for t in range(TT):
                        if s == S_DIVIDE[t]:
                            if t % 2 == 0:
                                sums(b, t // 2, n)
                            attention(b, t, n)
                    for k in range(CT):
                        if s == S_BACK[k] + 2:
                            dve.wait_ge(ath_done, CT * b + k + 1)
                            low_half(fi_ps[:, k, :], attTh[:, k, :], attTl[:, k, :], atl_done)
                    if s - 1 in S_OUT[1::2]:
                        k = S_OUT[1::2].index(s - 1)
                        dve.wait_ge(fi_full[k], fi_tasks(k, b, 6) + 1)
                        if k == 0:
                            dve.wait_ge(xb_done, b + 1)
                        if n >= 2:
                            dve.wait_ge(y_done, 2 * (b - 1) + k + 1)
                        r1, added = (buf[:, 2 * k:2 * k + 2, :].rearrange("p a c -> p (a c)") for buf in (res, xb))
                        nc.vector.tensor_tensor(r1, fi_ps[:, k, :], added, ALU.add).then_inc(r1_done, 1)
                    if s - 2 in S_OUT[1::2]:
                        k = S_OUT[1::2].index(s - 2)
                        dve.wait_ge(r1_done, 2 * b + k + 1)
                        stats_of(b, 0, res, 2 * k)
                    if n == NB and s in S_NORM:
                        last_norm(0, S_NORM.index(s), res, x1_done)
                    for k in range(CT):
                        if s == S_X1T[k] + 2:
                            dve.wait_ge(x1h_done, CT * b + k + 1)
                            low_half(fi_ps[:, k, :], x1h[:, k, :], x1l[:, k, :], x1l_done)
                    if s - 2 in S_UP[1::3]:
                        k = S_UP[1::3].index(s - 2)
                        dve.wait_ge(th_done, NH * b + k + 1)
                        nc.vector.scalar_tensor_tensor(th[:, k % 2, :], th[:, k % 2, :], 1.0, up_bank(n, k, 0),
                                                       ALU.add, ALU.mult).then_inc(pg_done, 1)
                    if s - 2 in S_UP[2::3]:
                        k = S_UP[2::3].index(s - 2)
                        dve.wait_ge(fi_full[1], fi_tasks(1, b, 11 + 2 * k) + 1)
                        dve.wait_ge(pg_done, NH * b + k + 1)
                        if k == 0 and project:
                            dve.wait_ge(p3_done, 4 * (i + 1) + 4)
                        if k >= 2 or n > 1:
                            dve.wait_ge(hl_done, NH * b + k - 1)
                        nc.vector.tensor_tensor(hf[:, k % 2, :], up_bank(n, k, 1), th[:, k % 2, :],
                                                ALU.mult).then_inc(hf_done, 1)
                if n == NB:
                    dve.wait_ge(hh_done, NH * NB)
                    dve.wait_ge(hl_done, NH * NB - 1)
                    nc.vector.tensor_tensor(hl[:, NH - 1, :], hf[:, (NH - 1) % 2, :], hh[:, NH - 1, :].bitcast(F32),
                                            ALU.subtract).then_inc(hl_done, 1)
                if finish:
                    if n >= 2:
                        dve.wait_ge(stored, 32 * (i - 1))
                    for k in range(2):
                        down(i, b, k, n)

            def norm2(b, s):
                if s in S_STATS2:
                    k = S_STATS2.index(s)
                    dve.wait_ge(r2_done, 2 * b + k + 1)
                    stats_of(b, 1, res, 2 * k)
                if s == S_MEAN2:
                    mean_var(b, 1)

            def sums(b, pair, n):
                for k in range(2):
                    dve.wait_ge(fi_full[k], fi_tasks(k, b, 2 * pair + k) + 1)
                banks = turn_banks(n, pair).rearrange("p k (h c) -> p k h c", c=2 * DH)
                nc.vector.tensor_scalar(den[:, :, :], banks[:, :, :, DH], EPS_DEN, None, ALU.add).then_inc(norm_step, 1)
                dve.wait_ge(norm_step, 4 * b + 2 * pair + 1)
                nc.vector.reciprocal(rden[:, :, :], den[:, :, :]).then_inc(norm_step, 1)

            def attention(b, t, n):
                bank = turn_banks(n, t // 2)[:, t % 2, :].rearrange("p (h c) -> p h c", c=2 * DH)
                dve.wait_ge(norm_step, 4 * b + t // 2 * 2 + 2)
                nc.vector.tensor_tensor(att[:, t, :].rearrange("p (h d) -> p h d", d=DH), bank[:, :, 0:DH],
                                        rden[:, t % 2, :].unsqueeze(2).broadcast_to([P, H, DH]),
                                        ALU.mult).then_inc(att_done, 1)

            def down(i, b, k, n):
                dve.wait_ge(fi_full[k], fi_tasks(k, b, 22) + 1)
                nc.vector.scalar_tensor_tensor(
                    res[:, 2 * k:2 * k + 2, :].rearrange("p a c -> p (a c)"), down_bank(n, k), 0.5 * W_SCALE ** 3,
                    res[:, 2 * k:2 * k + 2, :].rearrange("p a c -> p (a c)"), ALU.mult, ALU.add).then_inc(r2_done, 1)

            iterations(dve, body)
            for s in range(S_MEAN2 + 1):
                if s == S_MEAN2:
                    dve.wait_ge(st_done, 4 * NB)
                norm2(NB - 1, s)
            for half in range(2):
                last_norm(1, half, att, y_done)

        @block.tensor
        def _(pe):
            mm = nc.tensor.matmul

            def weights(n0, n1):
                for n in range(n0, n1):
                    if n >= 2:
                        pe.wait_ge(w_done, n - 1)
                        pe.wait_ge(wl_done, min(n - 1, 4))
                    bank = fi_ps[:, n % 2, :]
                    for c in range(4):
                        if n < 4:
                            src = w_stage[:, n, c % 2, (c // 2) * P:(c // 2 + 1) * P]
                        elif n < 10:
                            r = (n - 4) % 3
                            src = i_stage[(n - 4) // 3].rearrange("p (a c) -> p a c", c=D)[
                                :, 2 * r + c % 2, (c // 2) * P:(c // 2 + 1) * P]
                        else:
                            half = (i_stage[2], res[:, :, :].rearrange("p a c -> p (a c)"))[c % 2]
                            hid = 2 * (n - 10) + c // 2
                            src = half[:, hid * P:(hid + 1) * P]
                        last = nc.tensor.transpose(bank[:, c * P:(c + 1) * P], src, ident[:, :])
                    last.then_inc(fi_full[n % 2], 1)

            def halves(out_, left, right, which):
                steps = [(a, b_, c) for a, b_ in ((1, 0), (0, 1), (0, 0)) for c in range(CT)]
                for k in which:
                    a, b_, c = steps[k]
                    last = mm(out_, left(a, c), right(b_, c), start=(k == 0), stop=(k == 5))
                return last

            def rowmax(b, nb, tile, par):
                j, t, Q = tile // TT % 4, tile % TT, tile // 16
                if nb < NB:
                    at = rm_at(nb, ("tile", tile))
                    if tile % 32 == 0:
                        pe.wait_ge(stacked[tile // 32], 192 * (b + 1))
                    if nb > 0 or at >= 2:
                        pe.wait_ge(rm_free, RM_PER * b + at - 1)
                    h = 4 * Q + j
                    mm(rm_ps[:, at % 2, :], qs[par][0:KQ, h, t * P:(t + 1) * P], ks[par][0:KQ, h, :],
                       start=True, stop=True).then_inc(rm_full, 1)
                if tile % 16 == MLAG - 1:
                    if Q:
                        m_turn(b, nb, Q - 1)
                    elif nb:
                        m_turn(b - 1, nb - 1, QUADS - 1)

            def m_turn(b, nb, Q):
                tb, at = turn_at(b, nb, Q)
                pe.wait_ge(m_split, QUADS * b + Q + 1)
                pe.wait_ge(rm_free, RM_PER * tb + at - 1)
                if nb == 0 and Q == 0:
                    pe.wait_ge(ready_d, 2)
                nc.tensor.transpose(rm_ps[:, at % 2, :].bitcast(BF16)[:, 0:P],
                                    mparts[:, :, :].rearrange("p a m -> p (a m)"), identb[:, :]).then_inc(rm_full, 1)

            def body(i, par, live, n):
                project, attend, finish = live
                b = i - 1
                if n == -1:
                    pe.wait_ge(ready, 2)
                for s in range(SLOTS):
                    if n == -1 and s in W_SLOTS:
                        if W_SLOTS[s][0] == 0:
                            pe.wait_ge(w_in[0], 64)
                        elif W_SLOTS[s][0] == 4:
                            pe.wait_ge(w_flt, 4)
                        weights(*W_SLOTS[s])
                        if W_SLOTS[s] == (0, 2):
                            pe.wait_ge(wl_done, 1)
                        elif W_SLOTS[s] == (2, 4):
                            pe.wait_ge(wl_done, 3)
                    rb, nb, tile = rowmax_of(i, n, s)
                    if 0 <= nb < NB or (nb == NB and tile == MLAG - 1):
                        rowmax(rb, nb, tile, par if nb == n else 1 - par)
                    if attend:
                        j, kt, Q = s % 4, s // 4 % TT, s // 16
                        h = 4 * Q + j
                        if n == 0 and s == 0:
                            pe.wait_ge(ready, 5)
                            pe.wait_ge(ones_in, 32)
                        if s % 16 == 0:
                            pe.wait_ge(mrow_in[Q], 16 * (i + 1))
                        if n > 0 or s >= 2:
                            pe.wait_ge(exp_done, SLOTS * i + s - 1)
                        mm(sc_ps[:, s % 2, :], ks[par][0:KM, h, kt * P:(kt + 1) * P], qs[par][0:KM, h, :],
                           start=True, stop=True).then_inc(sc_full, 1)
                        if s >= 3 + PVLAG and (s - 3 - PVLAG) % 4 == 0:
                            product(i, par, (s - 3 - PVLAG) // 4, n)
                    ps = project_slot(n, s)
                    if project and ps in S_XT:
                        k = S_XT.index(ps)
                        if k == 0:
                            pe.wait_ge(x_landed, 16 * (i + 2))
                            if n > -1:
                                pe.wait_ge(r_done, 4 * (i + 1))
                        else:
                            pe.wait_ge(xtl_done, CT * (i + 1) + k)
                        for t in range(TT):
                            last = nc.tensor.transpose(pr_ps[:, t * P:(t + 1) * P], x_in[:, t, k * P:(k + 1) * P],
                                                       ident[:, :])
                        last.then_inc(pr_full, 1)
                    if project and (ps in S_QK or ps in S_QK2):
                        first = ps in S_QK
                        m = (S_QK if first else S_QK2).index(ps)
                        if first:
                            pr_free(i, ("qk", m))
                            if n == -1 and m == 1:
                                pe.wait_ge(wl_done, 2)
                        w = (wqT, wkT)[m % 2]
                        last = halves(pr_ps[:, :], lambda a, c: w[:, a, c, (m // 2) * P:(m // 2 + 1) * P],
                                      lambda a, c: (xTh, xTl)[a][:, c, :], range(0, 3) if first else range(3, 6))
                        if not first:
                            last.then_inc(pr_full, 1)
                    if project and ps in S_V:
                        t = S_V.index(ps)
                        if t % 2 == 0:
                            pr_free(i, ("v", t // 2))
                        last = halves(pr_ps[:, (t % 2) * D:(t % 2 + 1) * D],
                                      lambda a, c: (xTh, xTl)[a][:, c, t * P:(t + 1) * P],
                                      lambda a, c: wvT[:, a, c, :], range(6))
                        if t % 2:
                            last.then_inc(pr_full, 1)
                    if not finish:
                        continue
                    for t in range(TT):
                        if s == S_TURN[t]:
                            if t == 0:
                                pe.wait_ge(ot_done, QUADS * i)
                            if t >= 2 and n < NB:
                                pe.wait_ge(att_done, TT * b + t - 1)
                            elif t < 2 and n > 1:
                                pe.wait_ge(r2_done, 2 * (b - 1) + t + 1)
                            elif n == 1 and t == 0:
                                pe.wait_ge(w_done, W_TASKS)
                            for Q in range(QUADS):
                                last = nc.tensor.transpose(turn_banks(n, t // 2)[:, t % 2, Q * P:(Q + 1) * P],
                                                           oT[:, Q, t * P:(t + 1) * P], ident[:, :])
                            last.then_inc(fi_full[t % 2], 1)
                    for c in range(CT):
                        if s == S_BACK[c]:
                            for t in range(TT):
                                if c == 0 and n == NB:
                                    pe.wait_ge(att_done, TT * b + t + 1)
                                elif c == 0 and t == 0:
                                    pe.wait_ge(att_done, TT * b + TT)
                                last = nc.tensor.transpose(fi_ps[:, c, t * P:(t + 1) * P], att[:, t, c * P:(c + 1) * P],
                                                           ident[:, :])
                            last.then_inc(fi_full[c], 1)
                    if s in S_OUT:
                        t = S_OUT.index(s)
                        if t == 0:
                            pe.wait_ge(atl_done, CT * b + CT)
                        last = halves(fi_ps[:, t // 2, (t % 2) * D:(t % 2 + 1) * D],
                                      lambda a, c: (attTh, attTl)[a][:, c, t * P:(t + 1) * P],
                                      lambda a, c: woT[:, a, c, :], range(6))
                        if t % 2:
                            last.then_inc(fi_full[t // 2], 1)
                    for c in range(CT):
                        if s == S_X1T[c]:
                            for t in range(TT):
                                if c == 0 and t % 2 == 0:
                                    pe.wait_ge(x1_done, 2 * b + t // 2 + 1)
                                last = nc.tensor.transpose(fi_ps[:, c, t * P:(t + 1) * P], res[:, t, c * P:(c + 1) * P],
                                                           ident[:, :])
                            last.then_inc(fi_full[c], 1)
                    if s in S_UP:
                        k, third = divmod(S_UP.index(s), 3)
                        for q in ((0, 1, 2), (3, 4, 5), (6, 7))[third]:
                            bank, c, a = q // 4, q // 2 % 2, q % 2
                            if k == 0 and q in (0, 2):
                                pe.wait_ge(x1l_done, CT * b + c + 1)
                            if q % 4 == 0 and k and n < NB:
                                pe.wait_ge((pg_done, hf_done)[bank], NH * b + k)
                            elif q % 4 == 0 and k >= 2:
                                pe.wait_ge((pg_done, hf_done)[bank], NH * b + k - 1)
                            last = mm(up_bank(n, k, bank), (wgT, wuT)[bank][:, c, k * P:(k + 1) * P],
                                      (x1h, x1l)[a][:, c, :], start=(q % 4 == 0), stop=(q % 4 == 3))
                            if q % 4 == 3:
                                last.then_inc(fi_full[bank], 1)
                    for q in range(len(S_DOWN)):
                        if n < NB and s == S_DOWN[q]:
                            down(i, n, q // 5, q % 5)
                    if n == NB and s in S_UP[8::3]:
                        for k in range(2):
                            down(i, n, k, S_UP[8::3].index(s))
                if n == NB:
                    for k in range(2):
                        down(i, n, k, NH - 2)
                if finish:
                    for k in range(2):
                        down(i, n, k, NH - 1)
                if attend:
                    product(i, par, 15, n)

            def pr_free(i, key):
                before = {at: k for k, at in PR_AT.items()}[PR_AT[key] - 1]
                if before[0] == "xt":
                    pe.wait_ge(xtl_done, CT * (i + 1) + CT)
                elif before[0] == "qk":
                    pe.wait_ge(r_done, 4 * (i + 1) + before[1] + 1)
                else:
                    pe.wait_ge(v_done, 2 * (i + 1) + before[1] + 1)

            def down(i, n, k, g):
                b = i - 1
                if g == 0 and n < NB:
                    pe.wait_ge((pg_done, hf_done)[k], NH * b + NH)
                if k == 0:
                    pe.wait_ge(hl_done, NH * b + g + 1)
                for t in (2 * k, 2 * k + 1):
                    for part in (hl, hh):
                        last = mm(down_bank(n, k)[:, (t % 2) * D:(t % 2 + 1) * D], part[:, g, t * P:(t + 1) * P],
                                  wdT[:, g, :], start=(g == 0 and t % 2 == 0 and part is hl),
                                  stop=(g == NH - 1 and t % 2 == 1 and part is hh), skip_group_check=True)
                if g == NH - 1:
                    last.then_inc(fi_full[k], 1)

            def product(i, par, g, n):
                Q, kt = g // TT, g % TT
                if g == 0:
                    pe.wait_ge(v_done, 2 * (i + 1))
                if kt == 0 and (Q or n > 0):
                    pe.wait_ge(ot_done, QUADS * i + Q)
                pe.wait_ge(exp_done, SLOTS * i + 4 * g + 4)
                for j in range(4):
                    last = mm(pv_ps[32 * j:32 * j + 32, :], v1[par][:, kt, 4 * Q + j, :], e[:, g % RING, j, :],
                              start=(kt == 0), stop=(kt == TT - 1), tile_position=(0, 32 * j))
                last.then_inc(pv_done, 1)

            iterations(pe, body)


_INS = ["L0_attn_x", "L0_attn_Wq", "L0_attn_Wk", "L0_attn_Wv", "L0_attn_Wo", "L0_attn_bo",
        "L0_ffn_w_gate", "L0_ffn_w_up", "L0_ffn_w_down"]


def kernel(**inputs):
    import numpy as _np
    import concourse.bacc as _bacc
    from concourse import mybir as _mybir
    from concourse.bass_utils import run_bass_kernel_spmd as _run

    nc = _bacc.Bacc("TRN2", target_bir_lowering=False, num_devices=1)
    arrays, args = {}, []
    for name in _INS:
        a = _np.ascontiguousarray(inputs[name])
        arrays[f"in_{name}_dram"] = a
        args.append(nc.dram_tensor(f"in_{name}_dram", a.shape, _mybir.dt.from_np(a.dtype), kind="ExternalInput").ap())
    out = nc.dram_tensor("out_0_dram", (NB, T, D), _mybir.dt.float32, kind="ExternalOutput").ap()
    layer_program(nc, *args, out)
    r = _run(nc, [arrays], core_ids=[0])
    return r.results[0]["out_0_dram"]
```
